# Optimizing a Trainium2 kernel written in Bass

```python
import numpy as np
import jax
import jax.numpy as jnp

def _softmax(x, axis=-1):
    return jax.nn.softmax(x, axis=axis)

def _gelu(x):
    return jax.nn.gelu(x, approximate=True)

def _silu(x):
    return jax.nn.silu(x)

def _sigmoid(x):
    return jax.nn.sigmoid(x)

def _layernorm(x, axis=-1, eps=1e-05):
    m = jnp.mean(x, axis=axis, keepdims=True)
    v = jnp.var(x, axis=axis, keepdims=True)
    return (x - m) / jnp.sqrt(v + eps)

def _scatter_add(tgt, idx, src, axis=0):
    return tgt.at[idx].add(src)

def _segment_sum(src, seg, n):
    return jax.ops.segment_sum(src, seg, n)
kernel_name = 'mk_adaln_d1_jaxref_r8_70cb84'

def setup_inputs(seed: int=0):
    np.random.seed(seed)
    _w = jnp.asarray

    def _L0_attn_setup():
        import jax, jax.numpy as jnp
        import numpy as np
        B, L, H, NH = (4, 256, 128, 8)
        DK = H // NH
        DV = H // NH
        CONV_K, FIR_S, FIR_L = (4, 3, 31)
        CMAX = 0.2
        EPS = 1e-05
        CHUNK = 32

        def _l2norm(x):
            return x * jax.lax.rsqrt(jnp.sum(x * x, -1, keepdims=True) + 1e-06)

        def _rms(x, w):
            return x * jax.lax.rsqrt(jnp.mean(x * x, -1, keepdims=True) + EPS) * w

        def _causal_conv(x, w):
            K = w.shape[1]
            l = x.shape[1]
            xp = jnp.pad(x, ((0, 0), (K - 1, 0), (0, 0)))
            return sum((xp[:, i:i + l, :] * w[:, i][None, None, :] for i in range(K)))

        def _fir(x, w):
            K = w.shape[-1]
            l = x.shape[1]
            xp = jnp.pad(x, ((0, 0), (K - 1, 0), (0, 0), (0, 0)))
            return sum((xp[:, i:i + l] * w[:, :, i][None, None] for i in range(K)))

        def _delta_rule_chunkwise(q, k, v, beta, chunk=CHUNK):
            b, h, Ln, dk = q.shape
            dv = v.shape[-1]
            n = Ln // chunk
            q = _l2norm(q)
            k = _l2norm(k)
            v = v * beta[..., None]
            kb = k * beta[..., None]
            rs = lambda t: t.reshape(b, h, n, chunk, t.shape[-1])
            qc, kc, vc, kbc = (rs(q), rs(k), rs(v), rs(kb))
            mask_incl = jnp.triu(jnp.ones((chunk, chunk), dtype=bool), 0)
            mask_strict = jnp.triu(jnp.ones((chunk, chunk), dtype=bool), 1)
            attn = jnp.where(mask_incl, 0.0, -(kbc @ jnp.swapaxes(kc, -1, -2)))
            for i in range(1, chunk):
                row = attn[..., i, :]
                upd = jnp.einsum('bhnj,bhnjk->bhnk', row, attn[..., :i])
                attn = attn.at[..., i, :i].add(upd)
            attn = attn + jnp.eye(chunk, dtype=attn.dtype)
            u = attn @ vc
            w = attn @ kbc
            mv = lambda t: jnp.moveaxis(t, 2, 0)

            def step(S, xs):
                q_i, k_i, u_i, w_i = xs
                attn_local = jnp.where(mask_strict, 0.0, q_i @ jnp.swapaxes(k_i, -1, -2))
                u_new = u_i - w_i @ S
                o_i = q_i @ S + attn_local @ u_new
                S = S + jnp.swapaxes(k_i, -1, -2) @ u_new
                return (S, o_i)
            S0 = jnp.zeros((b, h, dk, dv), dtype=q.dtype)
            S, o = jax.lax.scan(step, S0, (mv(qc), mv(kc), mv(u), mv(w)))
            o = jnp.moveaxis(o, 0, 2).reshape(b, h, Ln, dv)
            return (o, S)

        def _forward(hidden_states, Wq, Wk, Wv, Wb, conv_q_w, conv_k_w, conv_v_w, fir_short_w, fir_long_w, floor_W, floor_b, fus_W1, fus_b1, fus_W2, fus_b2, norm_pf_w, norm_o_w, Wo):
            b, l, _ = hidden_states.shape
            hs = hidden_states
            q_lin = jax.nn.silu(_causal_conv(hs @ Wq, conv_q_w))
            k_lin = jax.nn.silu(_causal_conv(hs @ Wk, conv_k_w))
            v_lin = jax.nn.silu(_causal_conv(hs @ Wv, conv_v_w))
            q = q_lin.reshape(b, l, NH, DK)
            k = k_lin.reshape(b, l, NH, DK)
            v_direct = v_lin.reshape(b, l, NH, DV)
            beta = jax.nn.sigmoid(hs @ Wb)
            delta_out_t, _ = _delta_rule_chunkwise(jnp.transpose(q, (0, 2, 1, 3)), jnp.transpose(k, (0, 2, 1, 3)), jnp.transpose(v_direct, (0, 2, 1, 3)), jnp.transpose(beta, (0, 2, 1)))
            delta_out = jnp.transpose(delta_out_t, (0, 2, 1, 3))
            local_short = _fir(v_direct, fir_short_w)
            local_long = _fir(v_direct, fir_long_w)
            floor = jax.nn.sigmoid(hs @ floor_W + floor_b) * CMAX
            fus = jax.nn.gelu(hs @ fus_W1 + fus_b1, approximate=False) @ fus_W2 + fus_b2
            fus = fus.reshape(b, l, NH, 4)
            p_value = jax.nn.sigmoid(fus[..., 3]) * (1.0 - floor)
            ctx = jax.nn.softmax(fus[..., :3], axis=-1) * (1.0 - p_value)[..., None]
            o = ctx[..., 0, None] * local_short + ctx[..., 1, None] * local_long + ctx[..., 2, None] * delta_out + p_value[..., None] * v_direct
            o = _rms(o, norm_pf_w)
            o = _rms(o, norm_o_w)
            return o.reshape(b, l, NH * DV) @ Wo
        key = jax.random.key(seed)
        ks = jax.random.split(key, 16)
        n = lambda k, shape, s=0.02: jax.random.normal(k, shape, jnp.float32) * s
        fus_b2 = jnp.zeros((NH * 4,), jnp.float32).at[3::4].set(4.0)
        return {'hidden_states': jax.random.normal(ks[0], (B, L, H), jnp.float32), 'Wq': n(ks[1], (H, H)), 'Wk': n(ks[2], (H, H)), 'Wv': n(ks[3], (H, H)), 'Wb': n(ks[4], (H, NH)), 'conv_q_w': n(ks[5], (H, CONV_K), 0.2), 'conv_k_w': n(ks[6], (H, CONV_K), 0.2), 'conv_v_w': n(ks[7], (H, CONV_K), 0.2), 'fir_short_w': n(ks[8], (NH, DV, FIR_S), 0.2), 'fir_long_w': n(ks[9], (NH, DV, FIR_L), 0.2), 'floor_W': n(ks[10], (H, NH)), 'floor_b': jnp.full((NH,), float(np.log(CMAX / (1 - CMAX))), jnp.float32), 'fus_W1': n(ks[11], (H, 2 * H)), 'fus_b1': jnp.zeros((2 * H,), jnp.float32), 'fus_W2': n(ks[12], (2 * H, NH * 4)), 'fus_b2': fus_b2, 'norm_pf_w': jnp.ones((DV,), jnp.float32), 'norm_o_w': jnp.ones((DV,), jnp.float32), 'Wo': n(ks[13], (H, H))}
    _L0_attn_in = _L0_attn_setup()

    def _L0_ffn_setup():
        import jax, jax.numpy as jnp
        import numpy as np
        import math
        B, S, D = (4, 256, 128)
        E, DFF = (16, 256)
        CAP_FACTOR = 2.0
        ROUTER_HIDDEN = 128
        CAPACITY = int(math.ceil(S * CAP_FACTOR / E))
        key = jax.random.key(seed)
        ks = jax.random.split(key, 6)

        def uinit(k, shape, fan_in):
            bound = math.sqrt(3.0) * math.sqrt(1.0 / 3.0) / math.sqrt(fan_in)
            return jax.random.uniform(k, shape, jnp.float32, -bound, bound)
        return {'hidden_states': jax.random.normal(ks[0], (B, S, D), jnp.float32), 'router_w1': jax.random.normal(ks[1], (D, ROUTER_HIDDEN), jnp.float32) / math.sqrt(D), 'router_w2': jax.random.normal(ks[2], (ROUTER_HIDDEN, E), jnp.float32) / math.sqrt(ROUTER_HIDDEN), 'w1': uinit(ks[3], (E, D, DFF), D), 'w2': uinit(ks[4], (E, D, DFF), D), 'w3': uinit(ks[5], (E, DFF, D), DFF)}
    _L0_ffn_in = _L0_ffn_setup()
    _L0_c = _w((lambda *s: np.random.randn(*s).astype(np.float32) * 0.05)(16, 128))
    _L0_wmod = _w((lambda *s: np.random.randn(*s).astype(np.float32) * 0.05)(128, 6 * 128) * 128 ** (-0.5))
    _d = {'L0_attn_hidden_states': _L0_attn_in['hidden_states'], 'L0_attn_Wq': _L0_attn_in['Wq'], 'L0_attn_Wk': _L0_attn_in['Wk'], 'L0_attn_Wv': _L0_attn_in['Wv'], 'L0_attn_Wb': _L0_attn_in['Wb'], 'L0_attn_conv_q_w': _L0_attn_in['conv_q_w'], 'L0_attn_conv_k_w': _L0_attn_in['conv_k_w'], 'L0_attn_conv_v_w': _L0_attn_in['conv_v_w'], 'L0_attn_fir_short_w': _L0_attn_in['fir_short_w'], 'L0_attn_fir_long_w': _L0_attn_in['fir_long_w'], 'L0_attn_floor_W': _L0_attn_in['floor_W'], 'L0_attn_floor_b': _L0_attn_in['floor_b'], 'L0_attn_fus_W1': _L0_attn_in['fus_W1'], 'L0_attn_fus_b1': _L0_attn_in['fus_b1'], 'L0_attn_fus_W2': _L0_attn_in['fus_W2'], 'L0_attn_fus_b2': _L0_attn_in['fus_b2'], 'L0_attn_norm_pf_w': _L0_attn_in['norm_pf_w'], 'L0_attn_norm_o_w': _L0_attn_in['norm_o_w'], 'L0_attn_Wo': _L0_attn_in['Wo'], 'L0_ffn_router_w1': _L0_ffn_in['router_w1'], 'L0_ffn_router_w2': _L0_ffn_in['router_w2'], 'L0_ffn_w1': _L0_ffn_in['w1'], 'L0_ffn_w2': _L0_ffn_in['w2'], 'L0_ffn_w3': _L0_ffn_in['w3'], 'L0_c': _L0_c, 'L0_wmod': _L0_wmod}
    _x0 = _d['L0_attn_hidden_states']
    _d['L0_attn_hidden_states'] = jax.random.normal(jax.random.fold_in(jax.random.key(seed), 1), (16, 512, 128), dtype=_x0.dtype)
    del _x0
    return _d

def reference(L0_attn_hidden_states, L0_attn_Wq, L0_attn_Wk, L0_attn_Wv, L0_attn_Wb, L0_attn_conv_q_w, L0_attn_conv_k_w, L0_attn_conv_v_w, L0_attn_fir_short_w, L0_attn_fir_long_w, L0_attn_floor_W, L0_attn_floor_b, L0_attn_fus_W1, L0_attn_fus_b1, L0_attn_fus_W2, L0_attn_fus_b2, L0_attn_norm_pf_w, L0_attn_norm_o_w, L0_attn_Wo, L0_ffn_router_w1, L0_ffn_router_w2, L0_ffn_w1, L0_ffn_w2, L0_ffn_w3, L0_c, L0_wmod):

    def _L0_attn_ref(hidden_states, Wq, Wk, Wv, Wb, conv_q_w, conv_k_w, conv_v_w, fir_short_w, fir_long_w, floor_W, floor_b, fus_W1, fus_b1, fus_W2, fus_b2, norm_pf_w, norm_o_w, Wo):
        import jax, jax.numpy as jnp
        import numpy as np
        B, L, H, NH = (4, 256, 128, 8)
        DK = H // NH
        DV = H // NH
        CONV_K, FIR_S, FIR_L = (4, 3, 31)
        CMAX = 0.2
        EPS = 1e-05
        CHUNK = 32

        def _l2norm(x):
            return x * jax.lax.rsqrt(jnp.sum(x * x, -1, keepdims=True) + 1e-06)

        def _rms(x, w):
            return x * jax.lax.rsqrt(jnp.mean(x * x, -1, keepdims=True) + EPS) * w

        def _causal_conv(x, w):
            K = w.shape[1]
            l = x.shape[1]
            xp = jnp.pad(x, ((0, 0), (K - 1, 0), (0, 0)))
            return sum((xp[:, i:i + l, :] * w[:, i][None, None, :] for i in range(K)))

        def _fir(x, w):
            K = w.shape[-1]
            l = x.shape[1]
            xp = jnp.pad(x, ((0, 0), (K - 1, 0), (0, 0), (0, 0)))
            return sum((xp[:, i:i + l] * w[:, :, i][None, None] for i in range(K)))

        def _delta_rule_chunkwise(q, k, v, beta, chunk=CHUNK):
            b, h, Ln, dk = q.shape
            dv = v.shape[-1]
            n = Ln // chunk
            q = _l2norm(q)
            k = _l2norm(k)
            v = v * beta[..., None]
            kb = k * beta[..., None]
            rs = lambda t: t.reshape(b, h, n, chunk, t.shape[-1])
            qc, kc, vc, kbc = (rs(q), rs(k), rs(v), rs(kb))
            mask_incl = jnp.triu(jnp.ones((chunk, chunk), dtype=bool), 0)
            mask_strict = jnp.triu(jnp.ones((chunk, chunk), dtype=bool), 1)
            attn = jnp.where(mask_incl, 0.0, -(kbc @ jnp.swapaxes(kc, -1, -2)))
            for i in range(1, chunk):
                row = attn[..., i, :]
                upd = jnp.einsum('bhnj,bhnjk->bhnk', row, attn[..., :i])
                attn = attn.at[..., i, :i].add(upd)
            attn = attn + jnp.eye(chunk, dtype=attn.dtype)
            u = attn @ vc
            w = attn @ kbc
            mv = lambda t: jnp.moveaxis(t, 2, 0)

            def step(S, xs):
                q_i, k_i, u_i, w_i = xs
                attn_local = jnp.where(mask_strict, 0.0, q_i @ jnp.swapaxes(k_i, -1, -2))
                u_new = u_i - w_i @ S
                o_i = q_i @ S + attn_local @ u_new
                S = S + jnp.swapaxes(k_i, -1, -2) @ u_new
                return (S, o_i)
            S0 = jnp.zeros((b, h, dk, dv), dtype=q.dtype)
            S, o = jax.lax.scan(step, S0, (mv(qc), mv(kc), mv(u), mv(w)))
            o = jnp.moveaxis(o, 0, 2).reshape(b, h, Ln, dv)
            return (o, S)

        def _forward(hidden_states, Wq, Wk, Wv, Wb, conv_q_w, conv_k_w, conv_v_w, fir_short_w, fir_long_w, floor_W, floor_b, fus_W1, fus_b1, fus_W2, fus_b2, norm_pf_w, norm_o_w, Wo):
            b, l, _ = hidden_states.shape
            hs = hidden_states
            q_lin = jax.nn.silu(_causal_conv(hs @ Wq, conv_q_w))
            k_lin = jax.nn.silu(_causal_conv(hs @ Wk, conv_k_w))
            v_lin = jax.nn.silu(_causal_conv(hs @ Wv, conv_v_w))
            q = q_lin.reshape(b, l, NH, DK)
            k = k_lin.reshape(b, l, NH, DK)
            v_direct = v_lin.reshape(b, l, NH, DV)
            beta = jax.nn.sigmoid(hs @ Wb)
            delta_out_t, _ = _delta_rule_chunkwise(jnp.transpose(q, (0, 2, 1, 3)), jnp.transpose(k, (0, 2, 1, 3)), jnp.transpose(v_direct, (0, 2, 1, 3)), jnp.transpose(beta, (0, 2, 1)))
            delta_out = jnp.transpose(delta_out_t, (0, 2, 1, 3))
            local_short = _fir(v_direct, fir_short_w)
            local_long = _fir(v_direct, fir_long_w)
            floor = jax.nn.sigmoid(hs @ floor_W + floor_b) * CMAX
            fus = jax.nn.gelu(hs @ fus_W1 + fus_b1, approximate=False) @ fus_W2 + fus_b2
            fus = fus.reshape(b, l, NH, 4)
            p_value = jax.nn.sigmoid(fus[..., 3]) * (1.0 - floor)
            ctx = jax.nn.softmax(fus[..., :3], axis=-1) * (1.0 - p_value)[..., None]
            o = ctx[..., 0, None] * local_short + ctx[..., 1, None] * local_long + ctx[..., 2, None] * delta_out + p_value[..., None] * v_direct
            o = _rms(o, norm_pf_w)
            o = _rms(o, norm_o_w)
            return o.reshape(b, l, NH * DV) @ Wo
        return _forward(hidden_states, Wq, Wk, Wv, Wb, conv_q_w, conv_k_w, conv_v_w, fir_short_w, fir_long_w, floor_W, floor_b, fus_W1, fus_b1, fus_W2, fus_b2, norm_pf_w, norm_o_w, Wo)

    def _L0_ffn_ref(hidden_states, router_w1, router_w2, w1, w2, w3):
        import jax, jax.numpy as jnp
        import numpy as np
        import math
        B, S, D = (4, 256, 128)
        E, DFF = (16, 256)
        CAP_FACTOR = 2.0
        ROUTER_HIDDEN = 128
        CAPACITY = int(math.ceil(S * CAP_FACTOR / E))
        b, s, d = hidden_states.shape
        e = w1.shape[0]
        cap = CAPACITY
        router_logits = jax.nn.silu(hidden_states @ router_w1) @ router_w2
        expert_probs = jax.nn.softmax(router_logits.transpose(0, 2, 1), axis=-1)
        expert_weights, token_indices = jax.lax.top_k(expert_probs, cap)
        expert_weights = expert_weights / (expert_weights.sum(-1, keepdims=True) + 1e-09)
        expert_inputs = jax.vmap(lambda h, i: h[i])(hidden_states, token_indices)
        gate = jax.nn.silu(jnp.einsum('becd,edf->becf', expert_inputs, w1))
        value = jnp.einsum('becd,edf->becf', expert_inputs, w2)
        expert_out = jnp.einsum('becf,efd->becd', gate * value, w3)
        weighted = expert_out * expert_weights[..., None]

        def combine(idx, vals):
            return jnp.zeros((s, d), vals.dtype).at[idx.reshape(-1)].add(vals.reshape(-1, d))
        output = jax.vmap(combine)(token_indices, weighted)
        return output
    x = L0_attn_hidden_states
    mod = (_silu(L0_c) @ L0_wmod).reshape(L0_c.shape[0], 6, 1, -1)
    sa, ca, ga, sb, cb, gb = (mod[:, 0], mod[:, 1], mod[:, 2], mod[:, 3], mod[:, 4], mod[:, 5])
    ga = (2 * (ga >= 0) - 1) * jnp.maximum(jnp.abs(ga), 0.25)
    gb = (2 * (gb >= 0) - 1) * jnp.maximum(jnp.abs(gb), 0.25)
    h = _layernorm(x, axis=-1) * (1 + ca) + sa
    x = x + ga * _L0_attn_ref(h, L0_attn_Wq, L0_attn_Wk, L0_attn_Wv, L0_attn_Wb, L0_attn_conv_q_w, L0_attn_conv_k_w, L0_attn_conv_v_w, L0_attn_fir_short_w, L0_attn_fir_long_w, L0_attn_floor_W, L0_attn_floor_b, L0_attn_fus_W1, L0_attn_fus_b1, L0_attn_fus_W2, L0_attn_fus_b2, L0_attn_norm_pf_w, L0_attn_norm_o_w, L0_attn_Wo)
    h = _layernorm(x, axis=-1) * (1 + cb) + sb
    x = x + gb * _L0_ffn_ref(h, L0_ffn_router_w1, L0_ffn_router_w2, L0_ffn_w1, L0_ffn_w2, L0_ffn_w3)
    return x

_drawn_inputs = setup_inputs


def setup_inputs(seed=0):
    import zlib

    import numpy as np

    out = dict(_drawn_inputs(seed))
    spreads = {'L0_attn_floor_b': (-1.3862943649291992, 0.6),
     'L0_attn_fus_b1': (0.0, 0.8),
     'L0_attn_norm_pf_w': (1.0, 0.6),
     'L0_attn_norm_o_w': (1.0, 0.6)}
    factors = {'L0_attn_Wq': 8.0,
     'L0_attn_Wk': 8.0,
     'L0_attn_Wb': 8.0,
     'L0_attn_conv_q_w': 8.0,
     'L0_attn_conv_k_w': 8.0,
     'L0_attn_fir_short_w': 8.0,
     'L0_attn_fir_long_w': 8.0,
     'L0_attn_floor_W': 8.0,
     'L0_attn_fus_W1': 8.0,
     'L0_attn_fus_W2': 8.0,
     'L0_ffn_router_w1': 8.0,
     'L0_ffn_router_w2': 8.0,
     'L0_ffn_w1': 8.0,
     'L0_ffn_w2': 8.0,
     'L0_ffn_w3': 8.0}
    for name, (base, spread) in spreads.items():
        noise = np.random.default_rng([zlib.crc32(name.encode()), seed]).standard_normal(out[name].shape)
        drawn = base * np.exp(spread * noise) if base else spread * noise
        out[name] = jnp.asarray(drawn.astype(out[name].dtype))
    for name, factor in factors.items():
        out[name] = (out[name] * factor).astype(out[name].dtype)
    return out
```

```python
from contextlib import ExitStack

import concourse.bass as bass
from concourse import mybir

FP = mybir.dt.float32
U32 = mybir.dt.uint32
ALU = mybir.AluOpType
ACT = mybir.ActivationFunctionType
AXX = mybir.AxisListType.X

P = 128
NB, S, D = 16, 512, 128
NH, DH = 8, 16
C = 32
NCH = S // C
NJ = S // P
TAPS, FIR_S, FIR_L = 4, 3, 31
NF = 256
NG = 4
E, DFF, CAP, RH = 16, 256, 32, 128
NQ, G2 = 4, 2
NI = NB * G2
BAND = 2 * P - 1
LN_EPS = RMS_EPS = 1e-5
L2_EPS = 1e-6
CMAX = 0.2
SA, CA, GA, SB_, CB, GB = range(6)
K_T, B_T, Q_T, V_T = range(4)
CHG = 8
NCG = D // CHG


def cut(t, start, n):
    return t[:, start:start + n] if isinstance(start, int) else t[:, bass.ds(start, n)]


def steps(eng, n, body, first=2):
    for t in range(first):
        body(t, t % 2)
    with eng.Fori(first // 2, n // 2) as i:
        for u in range(2):
            body(i * 2 + u, u)


def after(eng, sem, t, ago, per=1, at=None, alone=False):
    if isinstance(t, int) and t < ago:
        return
    eng.wait_ge(sem, (t - ago) * per + (per if at is None else at))
    if alone and not isinstance(t, int):
        eng.nop(nofuse=True)


def landed(eng, sems, t, u, dmas=1):
    eng.wait_ge(sems[u], (t - u + 2) * 8 * dmas)


class Ctx:

    def __init__(self, nc, stack):
        self.nc, self.stack = nc, stack

    def sb(self, name, shape, dt=FP):
        return self.stack.enter_context(self.nc.sbuf_tensor(name, shape, dt))

    def ps(self, name):
        return self.stack.enter_context(self.nc.psum_tensor(name, [P, 512], FP))

    def sem(self, name):
        return self.stack.enter_context(self.nc.semaphore(name))


def stage_setup(nc, g, a):
    DRAWN = 5 + 3 * NQ + NB // 2 - 1
    with ExitStack() as stack:
        k = Ctx(nc, stack)
        xt = g.seqs[:, V_T * NB * S:(V_T + 1) * NB * S]
        c_in = k.sb("c_in", [NB, D])
        c_act = k.sb("c_act", [D, NB])
        wmod = k.sb("wmod_sb", [D, 6 * D])
        stats = k.sb("stats", [P, NB * NJ, 6])
        spread = k.sb("spread", [P, NB * NJ])
        sign = k.sb("sign", [P, 2, NB])
        size = k.sb("size", [P, 2, NB])
        gates_row = k.sb("gates_row", [NB, 2, D])
        band = k.sb("band", [P, BAND])
        band_ready, band_out = k.sem("band_ready"), k.sem("band_out")
        ps_c, ps_mod, ps_row = k.ps("ps_c"), k.ps("ps_mod"), k.ps("ps_row")
        w_in, c_ready = k.sem("w_in"), k.sem("c_ready")
        x_in = [k.sem(f"x_in{n}") for n in range(4)]
        cleared, drawn, c_turned, c_silu = k.sem("cleared"), k.sem("drawn"), k.sem("c_turned"), k.sem("c_silu")
        mod_ready, dve_done, var_ready, dev_ready = k.sem("mod_ready"), k.sem("dve_done0"), k.sem("var_ready"), k.sem("dev_ready")
        gate_ready, row_ready, row_copied, rows_moved = k.sem("gate_ready"), k.sem("row_ready"), k.sem("row_copied"), k.sem("rows_moved")
        stat_done = k.sem("stat_done")
        block = stack.enter_context(nc.Block())

        @block.sync
        def _(sp):
            sp.dma_start(c_in[:, :], a.c).then_inc(c_ready, 16)
            sp.dma_start(wmod[:, :], a.wmod).then_inc(c_ready, 16)
            for n in range(4):
                sp.dma_start(xt[:, n * 2048:(n + 1) * 2048].rearrange("p (m d) -> p m d", d=D),
                             a.x[4 * n:4 * n + 4].rearrange("b (j p) d -> p (b j) d", p=P)).then_inc(x_in[n], 16)
            sp.wait_ge(band_ready, 2)
            sp.dma_start(a.band, band[:, :]).then_inc(band_out, 16)
            sp.wait_ge(band_out, 16)
            for n in range(4):
                rows = slice(n * P // 4, (n + 1) * P // 4)
                sp.dma_start(a.toeplitz_near.rearrange("s c t -> c s t")[rows], a.window_near[rows]).then_inc(g.toeplitz, 16)
            sp.dma_start(a.toeplitz_far.rearrange("s c t -> c s t"), a.window_far).then_inc(g.toeplitz, 16)
            sp.wait_ge(row_copied, 1)
            sp.dma_start(a.gate_rows.rearrange("k b d -> b k d"), gates_row[:, :, :]).then_inc(rows_moved, 16)
            sp.wait_ge(rows_moved, 16)
            for bp in range(4):
                sp.dma_start(g.gb_rows[32 * bp:32 * bp + 32, :, :, :],
                             a.gate_rows[1].rearrange("(t h e) d -> h t e d", t=2, h=4)[bp:bp + 1]
                             .broadcast_to([32, 2, 2, D])).then_inc(rows_moved, 16)
            sp.wait_ge(rows_moved, 16 * 5)

        @block.scalar
        def _(act):
            n = 0
            for dst, src in g.weights:
                act.dma_start(dst, src, allow_slow_non_contiguous=True).then_inc(w_in, 16)
                n += 1
            act.wait_ge(c_turned, 1)
            act.activation(c_act[:, :], ps_c[:, 0:NB], ACT.Silu).then_inc(c_silu, 1)
            act.wait_ge(var_ready, 1)
            act.activation(spread[:, :], g.rstd[:, :], ACT.Sqrt, bias=g.eps_ln[:, :]).then_inc(dev_ready, 1)
            act.wait_ge(row_ready, 1)
            act.activation(gates_row[:, :, :], ps_row[0:NB, 0:2 * D].rearrange("b (k d) -> b k d", k=2),
                           ACT.Copy).then_inc(row_copied, 1)
            act.wait_ge(w_in, 16 * n)

        @block.gpsimd
        def _(pool):
            pool.memset(g.ident[:, :], 0.0).then_inc(cleared, 1)
            pool.memset(g.head_ones[:, :], 1.0).then_inc(cleared, 1)
            pool.memset(g.causal[:, :], 1.0).then_inc(cleared, 1)
            pool.memset(g.pair_mask[:, :], 1.0).then_inc(cleared, 1)
            pool.memset(g.item_mask[:, :], 1.0).then_inc(cleared, 1)
            pool.memset(g.eps_l2[:, :], L2_EPS).then_inc(cleared, 1)
            pool.memset(g.eps_ln[:, :], LN_EPS).then_inc(g.constants, 1)
            pool.wait_ge(cleared, 6)
            pool.wait_ge(g.constants, 1)
            count = 0

            def draw(out, src, op, fill, base, pattern, mult):
                nonlocal count
                pool.affine_select(out=out, in_=src, compare_op=op, fill=fill, base=base, pattern=pattern,
                                   channel_multiplier=mult).then_inc(drawn, 1)
                count += 1
                pool.wait_ge(drawn, count)

            draw(g.ident[:, :], g.ident[:, :], ALU.not_equal, 1.0, 0, [[-1, P]], 1)
            v = g.head_ones[:, :].rearrange("p (h d) -> p h d", d=DH)
            draw(v, v, ALU.is_ge, 0.0, 0, [[-DH, NH], [0, DH]], 1)
            draw(v, v, ALU.is_ge, 0.0, DH - 1, [[DH, NH], [0, DH]], -1)
            m = g.item_mask[:, :].rearrange("p (g q) -> p g q", g=G2)
            draw(m, m, ALU.is_ge, 0.0, 0, [[-DH, G2], [-32, NQ]], 1)
            draw(m, m, ALU.is_ge, 0.0, DH - 1, [[DH, G2], [32, NQ]], -1)
            for q in range(NQ):
                r = g.causal[32 * q:32 * q + 32, :]
                draw(r, r, ALU.is_ge, 0.0, 0, [[1, C]], -1)
                r = g.pair_mask[32 * q:32 * q + 32, :].rearrange("p (g d) -> p g d", g=G2)
                draw(r, r, ALU.is_ge, 0.0, 0, [[-DH, G2], [0, DH]], 1)
                draw(r, r, ALU.is_ge, 0.0, DH - 1, [[DH, G2], [0, DH]], -1)
            pool.wait_ge(stat_done, 1)
            for n in range(1, NB // 2):
                draw(g.row_step[:, n - 1:n], g.full_s[:, :], ALU.is_ge, 0.0, -E * n, [[0, 1]], 1)
            assert count == DRAWN

        @block.tensor
        def _(pe):
            pe.wait_ge(c_ready, 32)
            pe.wait_ge(drawn, 1)
            pe.transpose(ps_c[:, 0:NB], c_in[:, :], g.ident[0:NB, 0:NB]).then_inc(c_turned, 1)
            pe.wait_ge(c_silu, 1)
            for n in range(6):
                last = pe.matmul(ps_mod[:, n * NB:(n + 1) * NB], wmod[:, n * D:(n + 1) * D], c_act[:, :],
                                 start=True, stop=True)
            last.then_inc(mod_ready, 1)
            pe.wait_ge(gate_ready, 1)
            for n, which in enumerate((GA, GB)):
                last = pe.transpose(ps_row[0:NB, n * D:(n + 1) * D], g.mod[:, which, :], g.ident[:, :])
            last.then_inc(row_ready, 1)

        @block.vector
        def _(dve):
            dve.memset(g.full_s[:, :], float(S)).then_inc(stat_done, 1)
            for n in range(4):
                dve.wait_ge(x_in[n], 16)
                for m in range(16 * n, 16 * n + 16):
                    dve.bn_stats(stats[:, m, :], xt[:, m * D:(m + 1) * D]).then_inc(stat_done, 1)
            dve.wait_ge(stat_done, 1 + NB * NJ)
            done = 0

            def then(ins):
                nonlocal done
                done += 1
                ins.then_inc(dve_done, 1)
                dve.wait_ge(dve_done, done)

            then(dve.tensor_tensor(g.mean[:, :], stats[:, :, 1], stats[:, :, 4], ALU.add))
            then(dve.tensor_tensor(spread[:, :], stats[:, :, 1], stats[:, :, 4], ALU.subtract))
            then(dve.tensor_scalar(g.mean[:, :], g.mean[:, :], 0.5, None, ALU.mult))
            then(dve.tensor_tensor(spread[:, :], spread[:, :], spread[:, :], ALU.mult))
            then(dve.tensor_tensor(g.rstd[:, :], stats[:, :, 2], stats[:, :, 5], ALU.add))
            then(dve.tensor_scalar(spread[:, :], spread[:, :], 0.25, None, ALU.mult))
            then(dve.scalar_tensor_tensor(g.rstd[:, :], g.rstd[:, :], 1.0 / D, spread[:, :], ALU.mult, ALU.add))
            dve.wait_ge(g.constants, 1)
            dve.engine_nop().then_inc(var_ready, 1)
            dve.wait_ge(mod_ready, 1)
            then(dve.tensor_copy(g.mod[:, :, :], ps_mod[:, 0:6 * NB].rearrange("p (k b) -> p k b", b=NB)))
            pair = g.mod[:, GA:6:3, :]
            then(dve.tensor_scalar(g.mod[:, CA:6:3, :], g.mod[:, CA:6:3, :], 1.0, None, ALU.add))
            then(dve.tensor_scalar(sign[:, :, :], pair, 0.0, 2.0, ALU.is_ge, ALU.mult))
            then(dve.scalar_tensor_tensor(size[:, :, :], pair, -1.0, pair, ALU.mult, ALU.max))
            then(dve.tensor_scalar(size[:, :, :], size[:, :, :], 0.25, None, ALU.max))
            then(dve.scalar_tensor_tensor(pair, sign[:, :, :], -1.0, size[:, :, :], ALU.add, ALU.mult))
            for n, which in enumerate((CB, SB_)):
                src = g.mod[:, which, :].rearrange("p (t b e) -> p t e b", t=2, e=2)
                then(dve.tensor_copy(g.mod_slot[:, n, :].rearrange("p (t e b) -> p t e b", t=2, e=2), src))
            dve.engine_nop().then_inc(gate_ready, 1)
            dve.wait_ge(dev_ready, 1)
            then(dve.reciprocal(g.rstd[:, :], spread[:, :]))
            dve.wait_ge(drawn, DRAWN)
            then(dve.reduce_sum(g.row_base[:, 0:1], g.row_step[:, :], AXX))
            then(dve.tensor_scalar(g.row_base[:, 1:2], g.row_base[:, 0:1], float(S * NB // 2), None, ALU.add))
            dve.memset(band[:, :], 0.0).then_inc(band_ready, 1)
            dve.wait_ge(band_ready, 1)
            dve.wait_ge(w_in, 16 * len(g.weights))
            dve.tensor_copy(band[:, P - 1:P - 1 + FIR_L], g.w_long[:, ::-1]).then_inc(band_ready, 1)
            dve.wait_ge(w_in, 16 * len(g.weights))
            then(dve.tensor_tensor(g.w_norm[:, 2:3], g.w_norm[:, 0:1], g.w_norm[:, 1:2], ALU.mult))
            then(dve.tensor_scalar(g.Wo[:, :], g.Wo[:, :], g.w_norm[:, 2:3], None, ALU.mult))
            then(dve.tensor_copy(g.Wb_wide[:, :].rearrange("p (h d) -> p h d", d=DH), g.Wb[:, :].unsqueeze(2).broadcast_to([P, NH, DH])))
            then(dve.tensor_tensor(g.pf_sq[:, :], g.pf_sq[:, :], g.pf_sq[:, :], ALU.mult))


def stage_project(nc, g, a):
    with ExitStack() as stack:
        k = Ctx(nc, stack)
        N = S
        xh = k.sb("xh", [P, N])
        hT = [k.sb(f"hT{u}", [P, N]) for u in range(2)]
        padded = [k.sb(f"padded_{n}", [P, TAPS - 1 + N]) for n in "qkv"]
        conv = [k.sb(f"conv_{n}", [P, N]) for n in "qkv"]
        sq = [[k.sb(f"silu_{n}{u}", [P, (FIR_S - 1 if n == "v" else 0) + N]) for n in "qkv"] for u in range(2)]
        square = [k.sb(f"square_{n}", [P, N]) for n in "qk"]
        norm = k.sb("norm", [P, 2, NJ, NH])
        norm_wide = k.sb("norm_wide", [P, 2, NJ, D])
        beta = k.sb("beta", [P, N])
        hid = k.sb("hid", [P, 2, N])
        short = k.sb("short", [P, N])
        tok = [k.sb(f"tok_{n}", [P, N]) for n in "vs"]
        logit = k.sb("logit", [P, NJ * 40])
        ps_x = k.ps("ps_x")
        ps_p = [k.ps(f"ps_{n}") for n in "qkv"]
        ps_f = [k.ps(f"ps_f{n}") for n in range(2)]
        ps_a, ps_b = k.ps("ps_a"), k.ps("ps_b")
        names = """xh_done xT_ready hT_ready proj_q proj_k proj_v beta_logit fus_hidden pad_q pad_k pad_v
                   conv_q conv_k conv_v silu_q silu_k silu_v tanh_done beta_done square_q square_k sums
                   roots recips recips_wide wide_q wide_k q_done k_done b_done v_done gelu_done short_done v_turned s_turned
                   v_copied s_copied logit_ready logit_copied v_out s_out logit_out conv_step short_step cleared_pad""".split()
        s = {n: k.sem(n) for n in names}
        block = stack.enter_context(nc.Block())
        seq = lambda which, b: cut(g.seqs, b * S + which * NB * S, S)
        Q, K, V = range(3)

        @block.vector
        def _(dve):
            for n in range(3):
                dve.memset(padded[n][:, 0:TAPS - 1], 0.0).then_inc(s["cleared_pad"], 1)
            for u in range(2):
                dve.memset(sq[u][V][:, 0:FIR_S - 1], 0.0).then_inc(s["cleared_pad"], 1)
            dve.wait_ge(s["cleared_pad"], 5)

            def normalise(t):
                after(dve, s["xT_ready"], t, 1)
                for j in range(NJ):
                    m = t * NJ + j
                    last = dve.tensor_scalar(xh[:, j * P:(j + 1) * P], cut(g.seqs, m * D + V_T * NB * S, D),
                                             cut(g.mean, m, 1), cut(g.rstd, m, 1), ALU.subtract, ALU.mult)
                last.then_inc(s["xh_done"], 1)

            def convolve(t):
                for i, n in enumerate("qkv"):
                    after(dve, s["pad_" + n], t, 0)
                    after(dve, s["silu_" + n], t, 1)
                    for tap in range(TAPS):
                        if tap:
                            after(dve, s["conv_step"], t, 0, 9, 3 * i + tap)
                            ins = dve.scalar_tensor_tensor(conv[i][:, :], padded[i][:, tap:tap + N], g.taps[:, i, tap:tap + 1],
                                                           conv[i][:, :], ALU.mult, ALU.add)
                        else:
                            ins = dve.tensor_scalar(conv[i][:, :], padded[i][:, 0:N], g.taps[:, i, 0:1], None, ALU.mult)
                        ins.then_inc(s["conv_step"] if tap < TAPS - 1 else s["conv_" + n], 1)

            def finish(t, u):
                after(dve, s["tanh_done"], t, 0)
                dve.tensor_scalar(beta[:, :], beta[:, :], 0.5, 0.5, ALU.mult, ALU.add).then_inc(s["beta_done"], 1)
                after(dve, s["silu_v"], t, 0)
                after(dve, s["s_turned"], t, 1)
                for tap in range(FIR_S):
                    src = sq[u][V][:, tap:tap + N]
                    if tap:
                        after(dve, s["short_step"], t, 0, FIR_S - 1, tap)
                        ins = dve.scalar_tensor_tensor(short[:, :], src, g.w_short[:, tap:tap + 1], short[:, :], ALU.mult, ALU.add)
                    else:
                        ins = dve.tensor_scalar(short[:, :], src, g.w_short[:, 0:1], None, ALU.mult)
                    ins.then_inc(s["short_step"] if tap < FIR_S - 1 else s["short_done"], 1)

            def scale(t, u):
                after(dve, s["roots"], t, 0)
                dve.reciprocal(norm[:, :, :, :], norm[:, :, :, :]).then_inc(s["recips"], 1)
                after(dve, s["recips"], t, 0)
                after(dve, s["wide_q"], t, 1)
                wide = norm_wide[:, :, :, :].rearrange("p w j d -> p (w j d)").rearrange("p (n d) -> p n d", d=DH)
                dve.tensor_copy(wide, norm[:, :, :, :].rearrange("p w j h -> p (w j h)").unsqueeze(2)
                                .broadcast_to([P, 2 * NJ * NH, DH])).then_inc(s["recips_wide"], 1)
                after(dve, s["wide_k"], t, 0)
                dve.tensor_tensor(seq(K_T, t), sq[u][K][:, :], ps_b[:, :], ALU.mult).then_inc(s["k_done"], 1)
                after(dve, s["wide_q"], t, 0)
                dve.tensor_tensor(seq(Q_T, t), sq[u][Q][:, :], ps_a[:, :], ALU.mult).then_inc(s["q_done"], 1)
                after(dve, s["k_done"], t, 0)
                after(dve, s["beta_done"], t, 0)
                dve.scalar_tensor_tensor(seq(B_T, t), seq(K_T, t), -1.0, beta[:, :], ALU.mult, ALU.mult).then_inc(s["b_done"], 1)

            normalise(0)
            convolve(0)

            def body(t, u, last=False):
                if not last:
                    normalise(t + 1)
                finish(t, u)
                if not last:
                    convolve(t + 1)
                scale(t, u)
            body(0, 0)
            body(1, 1)
            with dve.Fori(1, NB // 2 - 1) as i:
                body(i * 2, 0)
                body(i * 2 + 1, 1)
            body(NB - 2, 0)
            body(NB - 1, 1, True)

        @block.gpsimd
        def _(pool):
            def body(t, u):
                after(pool, s["beta_done"], t, 0)
                after(pool, s["silu_v"], t, 0)
                after(pool, s["xh_done"], t, 0)
                pool.tensor_tensor(seq(V_T, t), sq[u][V][:, FIR_S - 1:], beta[:, :], ALU.mult).then_inc(s["v_done"], 1)
            steps(pool, NB, body)

        @block.scalar
        def _(act):
            act.wait_ge(s["cleared_pad"], 5)

            def modulate(t, u):
                after(act, s["xT_ready"], t, 0, alone=True)
                after(act, s["logit_ready"], t, 2, alone=True)
                act.activation(hT[u][:, :], ps_x[:, :], ACT.Identity, bias=cut(g.mod_flat, t + SA * NB, 1),
                               scale=cut(g.mod_flat, t + CA * NB, 1)).then_inc(s["hT_ready"], 1)

            def pad(t):
                for i, n in enumerate("qkv"):
                    after(act, s["proj_" + n], t, 0, alone=True)
                    after(act, s["conv_" + n], t, 1, alone=True)
                    act.activation(padded[i][:, TAPS - 1:], ps_p[i][:, :], ACT.Copy).then_inc(s["pad_" + n], 1)

            def silus(t, u):
                for i, n in ((V, "v"), (K, "k"), (Q, "q")):
                    after(act, s["conv_" + n], t, 0, alone=True)
                    if i == V:
                        after(act, s["v_done"], t, 2, alone=True)
                        after(act, s["short_done"], t, 2, alone=True)
                        after(act, s["v_turned"], t, 2, alone=True)
                        dst = sq[u][V][:, FIR_S - 1:]
                    else:
                        after(act, s[n + "_done"], t, 2, alone=True)
                        dst = sq[u][i][:, :]
                    act.activation(dst, conv[i][:, :], ACT.Silu).then_inc(s["silu_" + n], 1)
                after(act, s["beta_logit"], t, 0, alone=True)
                after(act, s["b_done"], t, 1, alone=True)
                after(act, s["v_done"], t, 1, alone=True)
                act.activation(beta[:, :], ps_x[:, :], ACT.Tanh, scale=0.5).then_inc(s["tanh_done"], 1)
                for i, n in ((K, "k"), (Q, "q")):
                    after(act, s["silu_" + n], t, 0, alone=True)
                    after(act, s["sums"], t, 1, alone=True)
                    act.activation(square[i][:, :], sq[u][i][:, :], ACT.Square).then_inc(s["square_" + n], 1)

            def rest(t, u):
                after(act, s["fus_hidden"], t, 0, alone=True)
                after(act, s["logit_ready"], t, 1, alone=True)
                for m in range(2):
                    last = act.activation(hid[:, m, :], ps_f[m][:, :], ACT.Gelu, bias=g.fus_b1[:, m:m + 1])
                last.then_inc(s["gelu_done"], 1)
                after(act, s["sums"], t, 0, alone=True)
                after(act, s["wide_k"], t, 1, alone=True)
                act.activation(norm[:, :, :, :].rearrange("p w j h -> p (w j h)"), ps_a[:, 0:2 * NJ * NH], ACT.Sqrt,
                               bias=g.eps_l2[:, :]).then_inc(s["roots"], 1)
                for i, n, src in ((0, "v", ps_a), (1, "s", ps_b)):
                    after(act, s[n + "_turned"], t, 0, alone=True)
                    after(act, s[n + "_out"], t, 1, 16, alone=True)
                    act.activation(tok[i][:, :], src[:, :], ACT.Copy).then_inc(s[n + "_copied"], 1)
                after(act, s["logit_ready"], t, 0, alone=True)
                after(act, s["logit_out"], t, 1, 16, alone=True)
                act.activation(logit[:, :], ps_b[:, 0:NJ * 40], ACT.Copy).then_inc(s["logit_copied"], 1)

            modulate(0, 0)
            pad(0)

            def body(t, u, last=False):
                silus(t, u)
                if not last:
                    modulate(t + 1, 1 - u)
                    pad(t + 1)
                rest(t, u)
            body(0, 0)
            body(1, 1)
            with act.Fori(1, NB // 2 - 1) as i:
                body(i * 2, 0)
                body(i * 2 + 1, 1)
            body(NB - 2, 0)
            body(NB - 1, 1, True)

        @block.tensor
        def _(pe):
            def project(t, u):
                after(pe, s["xh_done"], t, 0)
                after(pe, s["tanh_done"], t, 1)
                for j in range(NJ):
                    last = pe.transpose(ps_x[:, j * P:(j + 1) * P], xh[:, j * P:(j + 1) * P], g.ident[:, :])
                last.then_inc(s["xT_ready"], 1)
                after(pe, s["hT_ready"], t, 0)
                for i, n in enumerate("qkv"):
                    after(pe, s["pad_" + n], t, 1)
                    pe.matmul(ps_p[i][:, :], g.Wqkv[:, i, :], hT[u][:, :], start=True, stop=True).then_inc(s["proj_" + n], 1)
                pe.matmul(ps_x[:, :], g.Wb_wide[:, :], hT[u][:, :], start=True, stop=True).then_inc(s["beta_logit"], 1)
                after(pe, s["gelu_done"], t, 1)
                for m in range(2):
                    last = pe.matmul(ps_f[m][:, :], g.fus_W1[:, m * P:(m + 1) * P], hT[u][:, :], start=True, stop=True)
                last.then_inc(s["fus_hidden"], 1)

            def reduce(t, u):
                after(pe, s["square_k"], t, 0)
                after(pe, s["square_q"], t, 0)
                after(pe, s["v_copied"], t, 1)
                for i in range(2):
                    for j in range(NJ):
                        col = (i * NJ + j) * NH
                        last = pe.matmul(ps_a[:, col:col + NH], square[i][:, j * P:(j + 1) * P], g.head_ones[:, 0:P:DH],
                                         start=True, stop=True)
                last.then_inc(s["sums"], 1)

            def widen(t, u):
                after(pe, s["recips_wide"], t, 0)
                after(pe, s["logit_copied"], t, 1)
                for i, n, ps in ((K, "k", ps_b), (Q, "q", ps_a)):
                    for j in range(NJ):
                        last = pe.matmul(ps[:, j * P:(j + 1) * P], norm_wide[:, i, j, :],
                                         g.ident[:, :], start=True, stop=True)
                    last.then_inc(s["wide_" + n], 1)

            def turn(t, u):
                widen(t, u)
                after(pe, s["q_done"], t, 0)
                for j in range(NJ):
                    last = pe.transpose(ps_a[:, j * P:(j + 1) * P],
                                        sq[u][V][:, FIR_S - 1 + j * P:FIR_S - 1 + (j + 1) * P], g.ident[:, :])
                last.then_inc(s["v_turned"], 1)
                after(pe, s["k_done"], t, 0)
                after(pe, s["short_done"], t, 0)
                for j in range(NJ):
                    last = pe.transpose(ps_b[:, j * P:(j + 1) * P], short[:, j * P:(j + 1) * P], g.ident[:, :])
                last.then_inc(s["s_turned"], 1)
                after(pe, s["s_copied"], t, 0)
                after(pe, s["gelu_done"], t, 0)
                for j in range(NJ):
                    rows = slice(j * P, (j + 1) * P)
                    pe.matmul(ps_b[:, 40 * j + 32:40 * j + 40], hT[u][:, rows], g.floor_W[:, :], start=True, stop=True)
                    for m in range(2):
                        last = pe.matmul(ps_b[:, 40 * j:40 * j + 32], hid[:, m, rows], g.fus_W2[:, m, :],
                                         start=(m == 0), stop=(m == 1))
                last.then_inc(s["logit_ready"], 1)

            project(0, 0)

            def body(t, u, last=False):
                reduce(t, u)
                if not last:
                    project(t + 1, 1 - u)
                turn(t, u)
            body(0, 0)
            body(1, 1)
            with pe.Fori(1, NB // 2 - 1) as i:
                body(i * 2, 0)
                body(i * 2 + 1, 1)
            body(NB - 2, 0)
            body(NB - 1, 1, True)

        @block.sync
        def _(sp):
            def body(t, u):
                after(sp, s["v_copied"], t, 0)
                sp.dma_start(cut(a.v_tok, t * N, N), tok[0][:, :]).then_inc(s["v_out"], 16)
                after(sp, s["s_copied"], t, 0)
                sp.dma_start(cut(a.s_tok, t * N, N), tok[1][:, :]).then_inc(s["s_out"], 16)
                after(sp, s["logit_copied"], t, 0)
                sp.dma_start(cut(a.logits, t * NJ * 40, NJ * 40), logit[:, :]).then_inc(s["logit_out"], 16)
            steps(sp, NB, body)
            for n in ("v_out", "s_out", "logit_out"):
                sp.wait_ge(s[n], 16 * NB)


def stage_delta(nc, g, a):
    with ExitStack() as stack:
        k = Ctx(nc, stack)
        W = NB * C
        kv = k.sb("kv", [P, 2 * W])
        bq = [k.sb(f"bq{u}", [P, 2 * W]) for u in range(2)]
        k_wide = k.sb("k_wide", [P, NB, NQ, C])
        bq_heads = k.sb("bq_heads", [P, NB, G2, 2, C])
        k_tok, v_tok = k.sb("k_tok", [P, W]), k.sb("v_tok", [P, W])
        L = k.sb("L", [P, C, C])
        T = k.sb("T", [P, C, C])
        prod = k.sb("prod", [P, C * C // 4])
        TT = [k.sb(f"TT{u}", [P, NI * C]) for u in range(2)]
        attn = [k.sb(f"attn{u}", [P, NI, C]) for u in range(2)]
        r = k.sb("r", [P, W])
        uu = k.sb("u", [P, W])
        state = k.sb("state", [P, W])
        gain = k.sb("gain", [P, W])
        o_ch = k.sb("o_ch", [P, W])
        gram = stack.enter_context(nc.psum_tensor("gram", [P, NI * 2 * C], FP))
        ps_r, ps_u, ps_s, ps_o = k.ps("ps_r"), k.ps("ps_u"), k.ps("ps_s"), k.ps("ps_o")
        names = """wide_zero wide_in kv_in bq_in gram_ready L_ready attn_ready k_ready v_ready T_unit solved TT_ready
                   r_ps r_ready u_ps u_ready s_ps o_ps gain_ready state_ready o_turned o_stored unit_step""".split()
        s = {n: k.sem(n) for n in names}
        SOLVE = 2 * (C - 1)
        BEFORE_R, BEFORE_GAIN = 4, 22
        quad = lambda q: slice(32 * q, 32 * q + 32)
        block = stack.enter_context(nc.Block())

        def chunks(eng, run):
            run(0, 0, 2)
            run(1, 1, 2)
            with eng.Fori(1, NCH // 2 - 1) as i:
                run(i * 2, 0, 2)
                run(i * 2 + 1, 1, 2)
            run(NCH - 2, 0, 1)
            run(NCH - 1, 1, 0)

        @block.scalar
        def _(act):
            by_seq = g.seqs[:, :].rearrange("p (m s) -> p m s", s=S)
            wide = lambda x: x.rearrange("p (b c) -> p b c", c=C)
            act.wait_ge(s["wide_zero"], 1)

            def chunk_of(which, t):
                rows = by_seq[:, which * NB:(which + 1) * NB, :]
                return rows[:, :, t * C:(t + 1) * C] if isinstance(t, int) else rows[:, :, bass.ds(t * C, C)]

            def load_gram(t):
                after(act, s["gram_ready"], t, 1, alone=True)
                for q in range(NQ):
                    act.activation(k_wide[quad(q), :, q, :], chunk_of(K_T, t)[quad(q)], ACT.Copy)
                for w, which in enumerate((B_T, Q_T)):
                    for n in range(G2):
                        last = act.activation(bq_heads[:, :, n, w, :], chunk_of(which, t), ACT.Copy,
                                              scale=g.pair_mask[:, n * DH:n * DH + 1])
                last.then_inc(s["wide_in"], 1)

            def load(t, u):
                after(act, s["k_ready"], t, 1, alone=True)
                after(act, s["v_ready"], t, 1, alone=True)
                act.activation(wide(kv[:, 0:W]), chunk_of(K_T, t), ACT.Copy)
                act.activation(wide(kv[:, W:]), chunk_of(V_T, t), ACT.Copy).then_inc(s["kv_in"], 1)
                after(act, s["o_ps"], t, 2, alone=True)
                act.activation(wide(bq[u][:, 0:W]), chunk_of(B_T, t), ACT.Copy)
                act.activation(wide(bq[u][:, W:]), chunk_of(Q_T, t), ACT.Copy).then_inc(s["bq_in"], 1)

            def store(t):
                after(act, s["o_turned"], t, 0, alone=True)
                act.activation(chunk_of(V_T, t), wide(o_ch[:, :]), ACT.Copy).then_inc(s["o_stored"], 1)

            load_gram(0)
            load(0, 0)
            load_gram(1)

            def run(t, u, follow):
                if not (isinstance(t, int) and t == 0):
                    store(t - 1)
                if follow > 0:
                    load(t + 1, 1 - u)
                if follow > 1:
                    load_gram(t + 2)
                after(act, s["u_ps"], t, 0, alone=True)
                after(act, s["o_ps"], t, 1, alone=True)
                act.activation(uu[:, :], ps_u[:, :], ACT.Copy).then_inc(s["u_ready"], 1)
            chunks(act, run)
            store(NCH - 1)

        @block.gpsimd
        def _(pool):
            pool.memset(k_wide[:, :, :, :], 0.0).then_inc(s["wide_zero"], 1)

            def body(t, u):
                after(pool, s["TT_ready"], t, 1, alone=True)
                pool.memset(T[:, :, :], 0.0).then_inc(s["unit_step"], 1)
                after(pool, s["unit_step"], t, 0, alone=True)
                pool.memset(T[:, :, :].rearrange("p i j -> p (i j)")[:, 0:C * C:C + 1], 1.0).then_inc(s["T_unit"], 1)
            steps(pool, NCH, body)

        @block.tensor
        def _(pe):
            def make_gram(t, half):
                if half == 0:
                    after(pe, s["wide_in"], t, 0, alone=True)
                    after(pe, s["L_ready"], t, 1, alone=True)
                    after(pe, s["attn_ready"], t, 1, alone=True)
                for b in range(half * NB // 2, (half + 1) * NB // 2):
                    item = b * G2 * 2 * C
                    last = pe.matmul(gram[:, item:item + G2 * 2 * C], k_wide[:, b, :, :].rearrange("p q c -> p (q c)"),
                                     bq_heads[:, b, :, :, :].rearrange("p n w c -> p (n w c)"), start=True, stop=True)
                if half == 1:
                    last.then_inc(s["gram_ready"], 1)

            def per_pair(ps, lhs, rhs, only_first=False):
                for b in range(NB):
                    for q in range(NQ):
                        last = pe.matmul(ps[quad(q), b * C:(b + 1) * C], lhs[quad(q), b * C:(b + 1) * C],
                                         rhs[quad(q), b * C:(b + 1) * C], start=(b == 0 or not only_first),
                                         stop=not only_first, skip_group_check=only_first)
                return last

            def per_item(ps, lhs, rhs, add=False):
                for n in range(NI):
                    for q in range(NQ):
                        last = pe.matmul(ps[quad(q), n * DH:(n + 1) * DH], lhs[quad(q), n * C:(n + 1) * C],
                                         rhs[quad(q), n * DH:(n + 1) * DH], start=not add, stop=True,
                                         skip_group_check=add)
                return last

            for t in range(2):
                make_gram(t, 0)
                make_gram(t, 1)

            def run(t, u, follow):
                after(pe, s["bq_in"], t, 0, alone=True)
                after(pe, s["r_ready"], t, 1, alone=True)
                after(pe, s["state_ready"], t, 0, alone=True)
                per_pair(ps_r, bq[u][:, 0:W], state).then_inc(s["r_ps"], 1)
                after(pe, s["o_turned"], t, 1, alone=True)
                per_pair(ps_o, bq[u][:, W:], state, only_first=True)
                after(pe, s["TT_ready"], t, 0, alone=True)
                after(pe, s["u_ready"], t, 1, alone=True)
                after(pe, s["r_ready"], t, 0, alone=True)
                per_item(ps_u, TT[u], r).then_inc(s["u_ps"], 1)
                if follow > 1:
                    make_gram(t + 2, 0)
                after(pe, s["gain_ready"], t, 1, alone=True)
                after(pe, s["k_ready"], t, 0, alone=True)
                after(pe, s["u_ready"], t, 0, alone=True)
                per_pair(ps_s, k_tok, uu).then_inc(s["s_ps"], 1)
                after(pe, s["attn_ready"], t, 0, alone=True)
                per_item(ps_o, attn[u][:, :, :].rearrange("p n c -> p (n c)"), uu, add=True).then_inc(s["o_ps"], 1)
                if follow > 1:
                    make_gram(t + 2, 1)
            chunks(pe, run)

        @block.vector
        def _(dve):
            dve.memset(state[:, :], 0.0).then_inc(s["state_ready"], 1)
            g4 = gram[:, :].rearrange("p (n w i) -> p w i n", w=2, i=C)

            def turn_kv(t):
                after(dve, s["kv_in"], t, 0)
                after(dve, s["s_ps"], t, 1)
                dve.transpose(k_tok[:, :], kv[:, 0:W]).then_inc(s["k_ready"], 1)
                after(dve, s["r_ready"], t, 1)
                dve.transpose(v_tok[:, :], kv[:, W:]).then_inc(s["v_ready"], 1)

            def take_gram(t, u):
                after(dve, s["gram_ready"], t, 0)
                after(dve, s["solved"], t, 1, SOLVE)
                dve.transpose(L[:, :, :], g4[:, 0, :, :]).then_inc(s["L_ready"], 1)
                after(dve, s["o_ps"], t, 2)
                dve.tensor_tensor(attn[u][:, :, :], gram[:, :].rearrange("p (n w i) -> p n w i", w=2, i=C)[:, :, 1, :],
                                  g.causal[:, :].unsqueeze(1).broadcast_to([P, NI, C]), ALU.mult).then_inc(s["attn_ready"], 1)

            def solve(t, first, last):
                for m in range(first, last):
                    rows, cols = C - 1 - m, m + 1
                    tmp = prod[:, 0:rows * cols].rearrange("p (i j) -> p i j", j=cols)
                    if m == 0:
                        after(dve, s["L_ready"], t, 0)
                        after(dve, s["T_unit"], t, 0)
                    else:
                        after(dve, s["solved"], t, 0, SOLVE, 2 * m)
                    dve.tensor_tensor(tmp, L[:, m + 1:, m:m + 1].broadcast_to([P, rows, cols]),
                                      T[:, m:m + 1, 0:cols].broadcast_to([P, rows, cols]), ALU.mult).then_inc(s["solved"], 1)
                    after(dve, s["solved"], t, 0, SOLVE, 2 * m + 1)
                    dve.tensor_tensor(T[:, m + 1:, 0:cols], T[:, m + 1:, 0:cols], tmp, ALU.add).then_inc(s["solved"], 1)

            def turn_back(t, u):
                after(dve, s["solved"], t, 0, SOLVE)
                after(dve, s["u_ps"], t, 2)
                dve.transpose(TT[u][:, :].rearrange("p (n i) -> p i n", i=C), T[:, :, :]).then_inc(s["TT_ready"], 1)

            turn_kv(0)
            take_gram(0, 0)
            solve(0, 0, C - 1)
            turn_back(0, 0)

            def run(t, u, follow):
                if follow > 0:
                    take_gram(t + 1, 1 - u)
                    solve(t + 1, 0, BEFORE_R)
                after(dve, s["r_ps"], t, 0)
                after(dve, s["v_ready"], t, 0)
                after(dve, s["u_ps"], t, 1)
                dve.tensor_tensor(r[:, :], v_tok[:, :], ps_r[:, :], ALU.add).then_inc(s["r_ready"], 1)
                if follow > 0:
                    solve(t + 1, BEFORE_R, BEFORE_GAIN)
                after(dve, s["s_ps"], t, 0)
                dve.tensor_tensor(gain[:, :].rearrange("p (b c) -> p b c", c=C), ps_s[:, :].rearrange("p (b c) -> p b c", c=C),
                                  g.pair_mask[:, :].unsqueeze(1).broadcast_to([P, NB, C]), ALU.mult).then_inc(s["gain_ready"], 1)
                after(dve, s["gain_ready"], t, 0)
                dve.tensor_tensor(state[:, :], state[:, :], gain[:, :], ALU.add).then_inc(s["state_ready"], 1)
                if follow > 0:
                    solve(t + 1, BEFORE_GAIN, C - 1)
                    turn_back(t + 1, 1 - u)
                    turn_kv(t + 1)
                after(dve, s["o_ps"], t, 0)
                after(dve, s["o_stored"], t, 1)
                dve.transpose(o_ch[:, :], ps_o[:, :]).then_inc(s["o_turned"], 1)
            chunks(dve, run)


def stage_fir(nc, g, a):
    with ExitStack() as stack:
        k = Ctx(nc, stack)
        M = NB * NJ
        v_all = g.seqs[:, 0:M * D].rearrange("p (m d) -> p m d", d=D)
        y_all = g.seqs[:, M * D:2 * M * D].rearrange("p (m d) -> p m d", d=D)
        v_tail = k.sb("v_tail", [C, M, D])
        near = [k.sb(f"near{u}", [P, CHG, P]) for u in range(2)]
        far = [k.sb(f"far{u}", [C, CHG, C]) for u in range(2)]
        v_step = [k.sb(f"v_step{u}", [P, CHG, M]) for u in range(2)]
        tail_step = [k.sb(f"tail_step{u}", [C, CHG, M]) for u in range(2)]
        ps = [k.ps(f"ps_y{u}") for u in range(2)]
        v_in, w_in = k.sem("v_in"), [k.sem(f"band_in{u}") for u in range(2)]
        staged, tail_staged, y_ready, y_stored = k.sem("staged"), k.sem("tail_staged"), k.sem("y_ready"), k.sem("y_stored")
        block = stack.enter_context(nc.Block())

        @block.sync
        def _(sp):
            for n in range(4):
                cols = slice(n * M * D // 4, (n + 1) * M * D // 4)
                sp.dma_start(g.seqs[:, cols], a.v_tok[:, cols]).then_inc(v_in, 16)
            sp.wait_ge(g.toeplitz, 16 * 5)
            sp.dma_start(v_tail[:, :, :], a.v_tok[P - C:P, :].rearrange("p (m d) -> p m d", d=D)).then_inc(v_in, 16)

            def body(t, u):
                after(sp, y_ready, t, 2)
                rows = a.toeplitz_near[:, t * CHG:(t + 1) * CHG, :] if isinstance(t, int) else a.toeplitz_near[:, bass.ds(t * CHG, CHG), :]
                sp.dma_start(near[u][:, :, :], rows).then_inc(w_in[u], 16)
                rows = a.toeplitz_far[:, t * CHG:(t + 1) * CHG, :] if isinstance(t, int) else a.toeplitz_far[:, bass.ds(t * CHG, CHG), :]
                sp.dma_start(far[u][:, :, :], rows).then_inc(w_in[u], 16)
            steps(sp, NCG, body)

        @block.gpsimd
        def _(pool):
            pool.wait_ge(v_in, 80)

            def body(t, u):
                after(pool, y_ready, t, 2)
                src = v_tail[:, :, t * CHG:(t + 1) * CHG] if isinstance(t, int) else v_tail[:, :, bass.ds(t * CHG, CHG)]
                pool.tensor_copy(tail_step[u][:, :, :], src.rearrange("p m c -> p c m")).then_inc(tail_staged, 1)
            steps(pool, NCG, body)

        @block.vector
        def _(dve):
            dve.wait_ge(v_in, 80)

            def body(t, u):
                after(dve, y_ready, t, 2)
                src = v_all[:, :, t * CHG:(t + 1) * CHG] if isinstance(t, int) else v_all[:, :, bass.ds(t * CHG, CHG)]
                dve.tensor_copy(v_step[u][:, :, :], src.rearrange("p m c -> p c m")).then_inc(staged, 1)
            steps(dve, NCG, body)

        @block.tensor
        def _(pe):
            def body(t, u):
                landed(pe, w_in, t, u, 2)
                after(pe, staged, t, 0)
                after(pe, tail_staged, t, 0)
                after(pe, y_stored, t, 2)
                for c in range(CHG):
                    out = ps[u][:, c * M:(c + 1) * M]
                    pe.matmul(out, near[u][:, c, :], v_step[u][:, c, :], start=True, stop=False, skip_group_check=True)
                    head = out[0:C, :].rearrange("p (b j) -> p b j", j=NJ)[:, :, 1:]
                    tail = tail_step[u][:, c, :].rearrange("p (b j) -> p b j", j=NJ)[:, :, 0:NJ - 1]
                    last = pe.matmul(head, far[u][:, c, :], tail, start=False, stop=True, skip_group_check=True)
                last.then_inc(y_ready, 1)
            steps(pe, NCG, body)

        @block.scalar
        def _(act):
            def body(t, u):
                after(act, y_ready, t, 0, alone=True)
                dst = y_all[:, :, t * CHG:(t + 1) * CHG] if isinstance(t, int) else y_all[:, :, bass.ds(t * CHG, CHG)]
                act.activation(dst, ps[u][:, :].rearrange("p (c m) -> p m c", m=M), ACT.Copy).then_inc(y_stored, 1)
            steps(act, NCG, body)


def stage_gates(nc, g, a):
    with ExitStack() as stack:
        k = Ctx(nc, stack)
        M = NB * NJ
        raw = k.sb("raw", [P, M, 40])
        z = k.sb("z", [P, M, NH, NG])
        e = k.sb("e", [P, M, NH, NG])
        zf = k.sb("zf", [P, M, NH])
        top = k.sb("top", [P, M, NH])
        loaded, ga_in, exp3, exp_p, exp_f = k.sem("logits_in"), k.sem("ga_in"), k.sem("exp_ctx"), k.sem("exp_p"), k.sem("exp_floor")
        step, shifted, biased = k.sem("gate_step"), k.sem("shifted"), k.sem("biased")
        block = stack.enter_context(nc.Block())

        @block.sync
        def _(sp):
            sp.dma_start(raw[:, :, :], a.logits.rearrange("p (m c) -> p m c", c=40)).then_inc(loaded, 16)
            sp.dma_start(g.ga_rows[:, :, :], a.gate_rows[0:1].broadcast_to([P, NB, D])).then_inc(ga_in, 16)
            sp.wait_ge(ga_in, 16)

        @block.scalar
        def _(act):
            act.wait_ge(biased, 2)
            act.activation(e[:, :, :, 3], z[:, :, :, 3], ACT.Exp, scale=-1.0).then_inc(exp_p, 1)
            act.activation(zf[:, :, :], zf[:, :, :], ACT.Exp, scale=-1.0).then_inc(exp_f, 1)
            act.wait_ge(shifted, 1)
            act.activation(e[:, :, :, 0:3], z[:, :, :, 0:3], ACT.Exp).then_inc(exp3, 1)

        @block.vector
        def _(dve):
            done = 0

            def then(ins):
                nonlocal done
                done += 1
                ins.then_inc(step, 1)
                dve.wait_ge(step, done)

            dve.wait_ge(loaded, 16)
            dve.tensor_tensor(z[:, :, :, :].rearrange("p m h k -> p m (h k)"), raw[:, :, 0:32],
                              g.fus_b2[:, :].unsqueeze(1).broadcast_to([P, M, 32]), ALU.add).then_inc(biased, 1)
            dve.tensor_tensor(zf[:, :, :], raw[:, :, 32:40],
                              g.floor_b[:, :].unsqueeze(1).broadcast_to([P, M, NH]), ALU.add).then_inc(biased, 1)
            dve.wait_ge(biased, 2)
            then(dve.tensor_tensor(top[:, :, :], z[:, :, :, 0], z[:, :, :, 1], ALU.max))
            then(dve.tensor_tensor(top[:, :, :], top[:, :, :], z[:, :, :, 2], ALU.max))
            for n in range(3):
                then(dve.tensor_tensor(z[:, :, :, n], z[:, :, :, n], top[:, :, :], ALU.subtract))
            dve.engine_nop().then_inc(shifted, 1)
            dve.wait_ge(exp_f, 1)
            then(dve.tensor_scalar(zf[:, :, :], zf[:, :, :], 1.0, None, ALU.add))
            then(dve.reciprocal(zf[:, :, :], zf[:, :, :]))
            then(dve.tensor_scalar(zf[:, :, :], zf[:, :, :], -CMAX, 1.0, ALU.mult, ALU.add))
            dve.wait_ge(exp_p, 1)
            then(dve.tensor_scalar(top[:, :, :], e[:, :, :, 3], 1.0, None, ALU.add))
            then(dve.reciprocal(top[:, :, :], top[:, :, :]))
            then(dve.tensor_tensor(g.gate[3][:, :, :], zf[:, :, :], top[:, :, :], ALU.mult))
            dve.wait_ge(exp3, 1)
            then(dve.tensor_tensor(top[:, :, :], e[:, :, :, 0], e[:, :, :, 1], ALU.add))
            then(dve.tensor_tensor(top[:, :, :], top[:, :, :], e[:, :, :, 2], ALU.add))
            then(dve.reciprocal(top[:, :, :], top[:, :, :]))
            then(dve.tensor_scalar(zf[:, :, :], g.gate[3][:, :, :], -1.0, 1.0, ALU.mult, ALU.add))
            then(dve.tensor_tensor(top[:, :, :], top[:, :, :], zf[:, :, :], ALU.mult))
            for n in range(3):
                then(dve.tensor_tensor(g.gate[n][:, :, :], e[:, :, :, n], top[:, :, :], ALU.mult))


def stage_mix(nc, g, a):
    with ExitStack() as stack:
        k = Ctx(nc, stack)
        N, R = S, NJ * NH
        o_in = k.sb("o_in", [P, N])
        v_in = [k.sb(f"v_in{u}", [P, N]) for u in range(2)]
        s_in = [k.sb(f"s_in{u}", [P, N]) for u in range(2)]
        x_in = [k.sb(f"x_in{u}", [P, N]) for u in range(2)]
        acc = k.sb("acc", [P, N])
        part = k.sb("part", [P, N])
        side = k.sb("side", [P, N])
        side2 = k.sb("side2", [P, N])
        squares = k.sb("squares", [P, N])
        sm = k.sb("sm", [P, 5, R])
        normed = k.sb("normed", [P, N])
        oT = k.sb("oT", [P, N])
        x1 = k.sb("x1", [P, N])
        st = k.sb("st", [P, NJ, 6])
        mv = k.sb("mv", [P, NJ, 2])
        dev = k.sb("dev", [P, NJ])
        xh = k.sb("xh2", [P, N])
        hT = k.sb("h2T", [P, N])
        rh = k.sb("rh", [P, N])
        lg = k.sb("lg", [E, N])
        ps_o, ps_t, ps_y, ps_h, ps_r1, ps_r2 = (k.ps(n) for n in ("pc_o", "pc_t", "pc_y", "pc_h", "pc_r1", "pc_r2"))
        names = """o_loaded o_turned side_ready acc_ready squared sums_ready root_ready normed_ready
                   n_turned oT_ready y_ready x1_ready x1_out stat_ready dev_root xh_ready xh_out x_turned h_ready
                   r1_ready rh_ready r2_ready lg_ready lg_out dstep pstep""".split()
        s = {n: k.sem("c_" + n) for n in names}
        vs_in, xs_in = ([k.sem(f"{n}_in{u}") for u in range(2)] for n in ("vs", "xs"))
        block = stack.enter_context(nc.Block())
        M = NB * NJ
        DCH = 11

        heads = lambda x: x.rearrange("p (r d) -> p r d", d=DH)
        tiles = lambda x: x.rearrange("p (j d) -> p j d", d=D)

        def weight(n, t):
            w = g.gate[n][:, :, :].rearrange("p m h -> p (m h)")
            return cut(w, t * R, R).unsqueeze(2).broadcast_to([P, R, DH])

        @block.sync
        def _(sp):
            def loads(t, u):
                after(sp, s["side_ready"], t, 2)
                sp.dma_start(v_in[u][:, :], cut(a.v_tok, t * N, N)).then_inc(vs_in[u], 16)
                sp.dma_start(s_in[u][:, :], cut(a.s_tok, t * N, N)).then_inc(vs_in[u], 16)
                after(sp, s["x1_ready"], t, 2)
                src = a.x[t:t + 1] if isinstance(t, int) else a.x[bass.ds(t, 1)]
                sp.dma_start(tiles(x_in[u][:, :]), src.rearrange("b (j p) d -> p (b j) d", p=P)).then_inc(xs_in[u], 16)

            def stores(t, u):
                after(sp, s["x1_ready"], t, 0)
                dst = a.out[t:t + 1] if isinstance(t, int) else a.out[bass.ds(t, 1)]
                sp.dma_start(dst.rearrange("b (j p) d -> p (b j) d", p=P), tiles(x1[:, :])).then_inc(s["x1_out"], 16)
                after(sp, s["xh_ready"], t, 0)
                dst = a.xh2[t:t + 1] if isinstance(t, int) else a.xh2[bass.ds(t, 1)]
                sp.dma_start(dst.rearrange("b (j p) d -> p (b j) d", p=P), tiles(xh[:, :])).then_inc(s["xh_out"], 16)
                after(sp, s["lg_ready"], t, 0)
                dst = a.route[t:t + 1] if isinstance(t, int) else a.route[bass.ds(t, 1)]
                sp.dma_start(dst.rearrange("b e s -> e (b s)"), lg[:, :]).then_inc(s["lg_out"], 16)

            loads(0, 0)
            loads(1, 1)
            stores(0, 0)
            loads(2, 0)
            stores(1, 1)
            with sp.Fori(1, NB // 2 - 1) as i:
                loads(i * 2 + 1, 1)
                stores(i * 2, 0)
                loads(i * 2 + 2, 0)
                stores(i * 2 + 1, 1)
            loads(NB - 1, 1)
            stores(NB - 2, 0)
            stores(NB - 1, 1)
            for n in ("x1_out", "xh_out", "lg_out"):
                sp.wait_ge(s[n], 16 * NB)

        @block.gpsimd
        def _(pool):
            def body(t, u):
                landed(pool, vs_in, t, u, 2)
                after(pool, s["acc_ready"], t, 1)
                pool.tensor_tensor(heads(side[:, :]), heads(s_in[u][:, :]), weight(0, t), ALU.mult).then_inc(s["pstep"], 1)
                pool.tensor_tensor(heads(side2[:, :]), heads(v_in[u][:, :]), weight(3, t), ALU.mult).then_inc(s["pstep"], 1)
                after(pool, s["pstep"], t, 0, 2)
                pool.tensor_tensor(side[:, :], side[:, :], side2[:, :], ALU.add).then_inc(s["side_ready"], 1)
            steps(pool, NB, body)

        def piped(eng, front, back):
            front(0, 0)

            def body(t, u, last=False):
                if not last:
                    front(t + 1, 1 - u)
                back(t, u)
            body(0, 0)
            body(1, 1)
            with eng.Fori(1, NB // 2 - 1) as i:
                body(i * 2, 0)
                body(i * 2 + 1, 1)
            body(NB - 2, 0)
            body(NB - 1, 1, True)

        @block.scalar
        def _(act):
            def front(t, u):
                after(act, s["o_turned"], t, 1, alone=True)
                act.activation(o_in[:, :], cut(g.seqs, t * S + V_T * NB * S, S), ACT.Copy).then_inc(s["o_loaded"], 1)
                after(act, s["acc_ready"], t, 0, alone=True)
                after(act, s["sums_ready"], t, 1, alone=True)
                act.activation(squares[:, :], acc[:, :], ACT.Square).then_inc(s["squared"], 1)
                after(act, s["sums_ready"], t, 0, alone=True)
                act.activation(sm[:, 4, :], sm[:, 3, :], ACT.Sqrt).then_inc(s["root_ready"], 1)

            def back(t, u):
                after(act, s["n_turned"], t, 0, alone=True)
                after(act, s["y_ready"], t, 1, alone=True)
                act.activation(oT[:, :], ps_t[:, :], ACT.Copy).then_inc(s["oT_ready"], 1)
                after(act, s["stat_ready"], t, 0, alone=True)
                act.activation(dev[:, :], mv[:, :, 1], ACT.Sqrt, bias=g.eps_ln[:, :]).then_inc(s["dev_root"], 1)
                after(act, s["x_turned"], t, 0, alone=True)
                after(act, s["r1_ready"], t, 1, alone=True)
                act.activation(hT[:, :], ps_h[:, :], ACT.Identity, bias=cut(g.mod_flat, t + SB_ * NB, 1),
                               scale=cut(g.mod_flat, t + CB * NB, 1)).then_inc(s["h_ready"], 1)
                after(act, s["r1_ready"], t, 0, alone=True)
                after(act, s["r2_ready"], t, 1, alone=True)
                act.activation(rh[:, :], ps_r1[:, :], ACT.Silu).then_inc(s["rh_ready"], 1)
                after(act, s["r2_ready"], t, 0, alone=True)
                after(act, s["lg_out"], t, 1, 16, alone=True)
                act.activation(lg[:, :], ps_r2[0:E, :], ACT.Copy).then_inc(s["lg_ready"], 1)
            piped(act, front, back)

        @block.tensor
        def _(pe):
            def turn(ps, src):
                for j in range(NJ):
                    last = pe.transpose(ps[:, j * P:(j + 1) * P], src[:, j * P:(j + 1) * P], g.ident[:, :])
                return last

            def front(t, u):
                after(pe, s["o_loaded"], t, 0)
                after(pe, s["dstep"], t, 1, DCH, 1)
                turn(ps_o, o_in).then_inc(s["o_turned"], 1)

            def back(t, u):
                after(pe, s["normed_ready"], t, 0)
                after(pe, s["oT_ready"], t, 1)
                turn(ps_t, normed).then_inc(s["n_turned"], 1)
                after(pe, s["oT_ready"], t, 0)
                after(pe, s["x1_ready"], t, 1)
                for j in range(NJ):
                    last = pe.matmul(ps_y[:, j * D:(j + 1) * D], oT[:, j * P:(j + 1) * P], g.Wo[:, :], start=True, stop=True)
                last.then_inc(s["y_ready"], 1)
                after(pe, s["xh_ready"], t, 0)
                after(pe, s["h_ready"], t, 1)
                turn(ps_h, xh).then_inc(s["x_turned"], 1)
                after(pe, s["h_ready"], t, 0)
                after(pe, s["rh_ready"], t, 1)
                pe.matmul(ps_r1[:, :], g.rw1[:, :], hT[:, :], start=True, stop=True).then_inc(s["r1_ready"], 1)
                after(pe, s["rh_ready"], t, 0)
                after(pe, s["lg_ready"], t, 1)
                pe.matmul(ps_r2[0:E, :], g.rw2[:, :], rh[:, :], start=True, stop=True).then_inc(s["r2_ready"], 1)
            piped(pe, front, back)

        @block.vector
        def _(dve):
            def chained(t, count):
                def then(ins):
                    nonlocal count
                    count += 1
                    ins.then_inc(s["dstep"], 1)
                    after(dve, s["dstep"], t, 0, DCH, count)
                return then

            def front(t, u):
                y_all = g.seqs[:, M * D:2 * M * D]
                then = chained(t, 0)
                after(dve, s["o_turned"], t, 0)
                after(dve, s["squared"], t, 1)
                after(dve, s["normed_ready"], t, 1)
                then(dve.tensor_tensor(heads(acc[:, :]), heads(ps_o[:, :]), weight(2, t), ALU.mult))
                then(dve.tensor_tensor(heads(part[:, :]), heads(cut(y_all, t * N, N)), weight(1, t), ALU.mult))
                then(dve.tensor_tensor(acc[:, :], acc[:, :], part[:, :], ALU.add))
                after(dve, s["side_ready"], t, 0)
                dve.tensor_tensor(acc[:, :], acc[:, :], side[:, :], ALU.add).then_inc(s["acc_ready"], 1)
                after(dve, s["squared"], t, 0)
                then(dve.tensor_reduce(sm[:, 0, :], heads(squares[:, :]), AXX, ALU.add))
                then(dve.tensor_tensor(heads(part[:, :]), heads(squares[:, :]),
                                       g.pf_sq[:, :].unsqueeze(1).broadcast_to([P, R, DH]), ALU.mult))
                then(dve.tensor_reduce(sm[:, 1, :], heads(part[:, :]), AXX, ALU.add))
                then(dve.tensor_scalar(sm[:, 0, :], sm[:, 0, :], 1.0 / DH, RMS_EPS, ALU.mult, ALU.add))
                then(dve.reciprocal(sm[:, 0, :], sm[:, 0, :]))
                then(dve.scalar_tensor_tensor(sm[:, 1, :], sm[:, 1, :], 1.0 / DH, sm[:, 0, :], ALU.mult, ALU.mult))
                then(dve.tensor_scalar(sm[:, 1, :], sm[:, 1, :], RMS_EPS, None, ALU.add))
                then(dve.reciprocal(sm[:, 2, :], sm[:, 1, :]))
                after(dve, s["root_ready"], t, 1)
                dve.tensor_tensor(sm[:, 3, :], sm[:, 0, :], sm[:, 2, :], ALU.mult).then_inc(s["sums_ready"], 1)
                after(dve, s["root_ready"], t, 0)
                after(dve, s["n_turned"], t, 1)
                dve.tensor_tensor(heads(normed[:, :]), heads(acc[:, :]), sm[:, 4, :].unsqueeze(2).broadcast_to([P, R, DH]),
                                  ALU.mult).then_inc(s["normed_ready"], 1)

            def back(t, u):
                after(dve, s["y_ready"], t, 0)
                after(dve, s["x1_out"], t, 1, 16)
                landed(dve, xs_in, t, u)
                row = g.ga_rows[:, :, :].rearrange("p b d -> p (b d)")
                row = cut(row, t * D, D).unsqueeze(1).broadcast_to([P, NJ, D])
                b = s["b_step"]
                K = NJ + 2
                dve.tensor_tensor(tiles(x1[:, :]), tiles(ps_y[:, :]), row, ALU.mult).then_inc(b, 1)
                after(dve, b, t, 0, K, 1)
                dve.tensor_tensor(x1[:, :], x1[:, :], x_in[u][:, :], ALU.add).then_inc(s["x1_ready"], 1)
                after(dve, s["x1_ready"], t, 0)
                for j in range(NJ):
                    dve.bn_stats(st[:, j, :], x1[:, j * D:(j + 1) * D]).then_inc(b, 1)
                after(dve, b, t, 0, K, 1 + NJ, alone=True)
                for j in range(NJ):
                    last = dve.bn_aggr(mv[:, j, :], st[:, j, :])
                last.then_inc(s["stat_ready"], 1)
                after(dve, s["dev_root"], t, 0)
                dve.reciprocal(dev[:, :], dev[:, :]).then_inc(b, 1)
                after(dve, b, t, 0, K, 2 + NJ)
                after(dve, s["x_turned"], t, 1)
                after(dve, s["xh_out"], t, 1, 16)
                for j in range(NJ):
                    last = dve.tensor_scalar(xh[:, j * D:(j + 1) * D], x1[:, j * D:(j + 1) * D], mv[:, j, 0:1],
                                             dev[:, j:j + 1], ALU.subtract, ALU.mult)
                last.then_inc(s["xh_ready"], 1)
            s["b_step"] = k.sem("c_b_step")
            piped(dve, front, back)


def stage_route(nc, g, a):
    with ExitStack() as stack:
        k = Ctx(nc, stack)
        lg = k.sb("route_lg", [P, 2, S])
        work = k.sb("route_work", [P, 2, S])
        junk = k.sb("route_exp", [P, 2, S])
        best = k.sb("best", [P, 2, CAP])
        at = k.sb("at", [P, 2, CAP], U32)
        atf = k.sb("atf", [P, 2, CAP])
        neg = k.sb("neg", [P, 2])
        tot = k.sb("tot", [P, 2])
        rest = k.sb("rest", [P, 2])
        turned = k.sb("turned", [P, 2, CAP])
        loaded, step, neg_ready, exp_ready = k.sem("route_in"), k.sem("route_step"), k.sem("neg_ready"), k.sem("exp_ready")
        block = stack.enter_context(nc.Block())

        @block.sync
        def _(sp):
            for t in range(2):
                sp.dma_start(lg[:, t, :], a.route[8 * t:8 * t + 8].rearrange("b e s -> (b e) s")).then_inc(loaded, 16)
            sp.wait_ge(loaded, 32)

        @block.scalar
        def _(act):
            act.wait_ge(neg_ready, 1)
            for t in range(2):
                act.activation(junk[:, t, :], lg[:, t, :], ACT.Exp, bias=neg[:, t:t + 1], accum_out=tot[:, t:t + 1])
            for t in range(2):
                last = act.activation(best[:, t, :], best[:, t, :], ACT.Exp, bias=neg[:, t:t + 1])
            last.then_inc(exp_ready, 1)

        @block.vector
        def _(dve):
            done = 0

            def then(*ins):
                nonlocal done
                done += len(ins)
                for x in ins:
                    x.then_inc(step, 1)
                dve.wait_ge(step, done)

            dve.wait_ge(loaded, 32)
            for r in range(CAP // 8):
                cols = slice(8 * r, 8 * r + 8)
                src = [(lg if r == 0 else work)[:, t, :] for t in range(2)]
                then(*[dve.max(best[:, t, cols], src[t]) for t in range(2)])
                then(*[dve.max_index(at[:, t, cols], best[:, t, cols], src[t]) for t in range(2)])
                if r < CAP // 8 - 1:
                    then(*[dve.match_replace(work[:, t, :], best[:, t, cols], src[t], -3.0e38) for t in range(2)])
            then(dve.tensor_scalar(neg[:, :], best[:, :, 0], -1.0, None, ALU.mult))
            dve.engine_nop().then_inc(neg_ready, 1)
            then(dve.tensor_copy(atf[:, :, :], at[:, :, :]))
            then(*[dve.tensor_scalar(atf[:, t, :], atf[:, t, :], g.row_base[:, t:t + 1], None, ALU.add) for t in range(2)])
            then(*[dve.transpose(turned[:, t, :], atf[:, t, :]) for t in range(2)])
            then(dve.tensor_copy(g.slot_row[:, :, :].rearrange("p e (t b) -> p t b e", t=2),
                                 turned[:, :, :].rearrange("p t (b e) -> p t b e", b=2)))
            dve.wait_ge(exp_ready, 1)
            then(dve.reciprocal(tot[:, :], tot[:, :]))
            then(*[dve.tensor_scalar(best[:, t, :], best[:, t, :], tot[:, t:t + 1], None, ALU.mult) for t in range(2)])
            then(dve.reduce_sum(rest[:, :], best[:, :, :], AXX))
            then(dve.tensor_scalar(rest[:, :], rest[:, :], 1e-9, None, ALU.add))
            then(dve.reciprocal(rest[:, :], rest[:, :]))
            then(*[dve.tensor_scalar(best[:, t, :], best[:, t, :], rest[:, t:t + 1], None, ALU.mult) for t in range(2)])
            then(*[dve.transpose(turned[:, t, :], best[:, t, :]) for t in range(2)])
            then(dve.tensor_copy(g.slot_w[:, :, :].rearrange("p e (t b) -> p t b e", t=2),
                                 turned[:, :, :].rearrange("p t (b e) -> p t b e", b=2)))


def stage_experts(nc, g, a):
    with ExitStack() as stack:
        k = Ctx(nc, stack)
        N = NB * CAP
        NGR = N // P
        w1 = [k.sb(f"w1_{u}", [D, DFF]) for u in range(2)]
        w2 = [k.sb(f"w2_{u}", [D, DFF]) for u in range(2)]
        w3 = [k.sb(f"w3_{u}", [P, 2, D]) for u in range(2)]
        rows = [k.sb(f"rows{u}", [P, NGR], U32) for u in range(2)]
        wts = [k.sb(f"wts{u}", [P, NGR]) for u in range(2)]
        got = [k.sb(f"got{u}", [P, N]) for u in range(2)]
        xT = k.sb("xT", [P, N])
        gu = k.sb("gu", [P, 2, N])
        act_g = k.sb("act_g", [P, 2, N])
        y = [k.sb(f"y{u}", [P, N]) for u in range(2)]
        ps_x, ps_y = k.ps("pe_x"), k.ps("pe_y")
        ps_g = [k.ps(f"pe_g{m}") for m in range(2)]
        ps_v = [k.ps(f"pe_v{m}") for m in range(2)]
        names = """rows_ready x_turned x_scaled x_ready gate_ready value_ready act_ready gu_ready y_ready
                   y_done added""".split()
        s = {n: k.sem("e_" + n) for n in names}
        w_in, got_in = ([k.sem(f"{n}_in{u}") for u in range(2)] for n in ("expert", "got"))
        block = stack.enter_context(nc.Block())
        groups = lambda x: x.rearrange("p (n c) -> p n c", c=CAP)
        flat_xh = a.xh2.rearrange("b s d -> (b s) d")
        flat_out = a.out.rearrange("b s d -> (b s) d")

        @block.sync
        def _(sp):
            def body(t, u):
                after(sp, s["y_ready"], t, 2)
                pick = lambda w: w[t:t + 1] if isinstance(t, int) else w[bass.ds(t, 1)]
                sp.dma_start(w1[u][:, :], pick(a.w1).rearrange("e d f -> d (e f)")).then_inc(w_in[u], 16)
                sp.dma_start(w2[u][:, :], pick(a.w2).rearrange("e d f -> d (e f)")).then_inc(w_in[u], 16)
                sp.dma_start(w3[u][:, :, :], pick(a.w3).rearrange("e (m p) d -> p (e m) d", p=P)).then_inc(w_in[u], 16)
            steps(sp, E, body)

        @block.gpsimd
        def _(pool):
            def pick_rows(t, u):
                after(pool, s["y_done"], t, 2, alone=True)
                if not (isinstance(t, int) and t < 2):
                    pool.wait_ge(s["added"], (t - 1) * 16 * NGR)
                pool.tensor_copy(rows[u][:, :], cut(g.slot_row_flat, t * NGR, NGR))
                pool.tensor_copy(wts[u][:, :], cut(g.slot_w_flat, t * NGR, NGR)).then_inc(s["rows_ready"], 1)

            def gather(t, u):
                pick_rows(t, u)
                after(pool, s["rows_ready"], t, 0, alone=True)
                after(pool, s["x_turned"], t, 2, alone=True)
                for n in range(NGR):
                    pool.indirect_dma_start(got[u][:, n * D:(n + 1) * D], None, flat_xh,
                                            bass.IndirectOffsetOnAxis(ap=rows[u][:, n:n + 1], axis=0))\
                        .then_inc(got_in[u], 16)

            def add(t, u):
                after(pool, s["y_done"], t, 0, alone=True)
                after(pool, s["added"], t, 1, 16 * NGR, alone=True)
                for n in range(NGR):
                    pool.indirect_dma_start(flat_out, bass.IndirectOffsetOnAxis(ap=rows[u][:, n:n + 1], axis=0),
                                            y[u][:, n * D:(n + 1) * D], None, compute_op=ALU.add)\
                        .then_inc(s["added"], 16)

            gather(0, 0)

            def body(t, u, last=False):
                if not last:
                    gather(t + 1, 1 - u)
                add(t, u)
            body(0, 0)
            body(1, 1)
            with pool.Fori(1, E // 2 - 1) as i:
                body(i * 2, 0)
                body(i * 2 + 1, 1)
            body(E - 2, 0)
            body(E - 1, 1, True)
            pool.wait_ge(s["added"], 16 * NGR * E)

        @block.tensor
        def _(pe):
            def fetch(t, u):
                landed(pe, got_in, t, u, NGR)
                after(pe, s["x_scaled"], t, 1)
                for n in range(NGR):
                    last = pe.transpose(ps_x[:, n * P:(n + 1) * P], got[u][:, n * D:(n + 1) * D], g.ident[:, :])
                last.then_inc(s["x_turned"], 1)

            def run(t, u, last_step):
                after(pe, s["x_ready"], t, 0)
                landed(pe, w_in, t, u, 3)
                after(pe, s["act_ready"], t, 1)
                for m in range(2):
                    last = pe.matmul(ps_g[m][:, :], w1[u][:, m * P:(m + 1) * P], xT[:, :], start=True, stop=True)
                last.then_inc(s["gate_ready"], 1)
                after(pe, s["gu_ready"], t, 1)
                for m in range(2):
                    last = pe.matmul(ps_v[m][:, :], w2[u][:, m * P:(m + 1) * P], xT[:, :], start=True, stop=True)
                last.then_inc(s["value_ready"], 1)
                if not last_step:
                    fetch(t + 1, 1 - u)
                after(pe, s["gu_ready"], t, 0)
                after(pe, s["y_done"], t, 1)
                for n in range(NGR):
                    for m in range(2):
                        last = pe.matmul(ps_y[:, n * D:(n + 1) * D], gu[:, m, n * P:(n + 1) * P], w3[u][:, m, :],
                                         start=(m == 0), stop=(m == 1))
                last.then_inc(s["y_ready"], 1)
            fetch(0, 0)
            run(0, 0, False)
            run(1, 1, False)
            with pe.Fori(1, E // 2 - 1) as i:
                run(i * 2, 0, False)
                run(i * 2 + 1, 1, False)
            run(E - 2, 0, False)
            run(E - 1, 1, True)

        @block.scalar
        def _(act):
            def body(t, u):
                after(act, s["gate_ready"], t, 0, alone=True)
                after(act, s["gu_ready"], t, 1, alone=True)
                for m in range(2):
                    last = act.activation(act_g[:, m, :], ps_g[m][:, :], ACT.Silu)
                last.then_inc(s["act_ready"], 1)
            steps(act, E, body)

        @block.vector
        def _(dve):
            cb = g.mod_slot[:, 0, :].unsqueeze(2).broadcast_to([P, NB, CAP])
            sb = g.mod_slot[:, 1, :].unsqueeze(2).broadcast_to([P, NB, CAP])

            def modulate(t):
                after(dve, s["x_turned"], t, 0)
                after(dve, s["value_ready"], t, 1)
                dve.tensor_tensor(groups(xT[:, :]), groups(ps_x[:, :]), cb, ALU.mult).then_inc(s["x_scaled"], 1)
                after(dve, s["x_scaled"], t, 0)
                dve.tensor_tensor(groups(xT[:, :]), groups(xT[:, :]), sb, ALU.add).then_inc(s["x_ready"], 1)

            def body(t, u, last_step=False):
                after(dve, s["act_ready"], t, 0)
                after(dve, s["value_ready"], t, 0)
                after(dve, s["y_ready"], t, 1)
                for m in range(2):
                    last = dve.tensor_tensor(gu[:, m, :], act_g[:, m, :], ps_v[m][:, :], ALU.mult)
                last.then_inc(s["gu_ready"], 1)
                if not last_step:
                    modulate(t + 1)
                after(dve, s["y_ready"], t, 0)
                after(dve, s["rows_ready"], t, 0)
                after(dve, s["added"], t, 2, 16 * NGR)
                for n in range(NGR):
                    last = dve.scalar_tensor_tensor(y[u][:, n * D:(n + 1) * D], ps_y[:, n * D:(n + 1) * D], wts[u][:, n:n + 1],
                                                    g.gb_rows[:, n // 2, n % 2, :], ALU.mult, ALU.mult)
                last.then_inc(s["y_done"], 1)
            modulate(0)
            body(0, 0)
            body(1, 1)
            with dve.Fori(1, E // 2 - 1) as i:
                body(i * 2, 0)
                body(i * 2 + 1, 1)
            body(E - 2, 0)
            body(E - 1, 1, True)


class Part:
    pass


def adaln_block_kernel(nc, L0_attn_hidden_states, L0_attn_Wq, L0_attn_Wk, L0_attn_Wv, L0_attn_Wb, L0_attn_conv_q_w,
                       L0_attn_conv_k_w, L0_attn_conv_v_w, L0_attn_fir_short_w, L0_attn_fir_long_w, L0_attn_floor_W,
                       L0_attn_floor_b, L0_attn_fus_W1, L0_attn_fus_b1, L0_attn_fus_W2, L0_attn_fus_b2,
                       L0_attn_norm_pf_w, L0_attn_norm_o_w, L0_attn_Wo, L0_ffn_router_w1, L0_ffn_router_w2,
                       L0_ffn_w1, L0_ffn_w2, L0_ffn_w3, L0_c, L0_wmod, out, upto=99):
    a, g = Part(), Part()
    a.x, a.c, a.wmod, a.out = L0_attn_hidden_states, L0_c, L0_wmod, out
    a.w1, a.w2, a.w3 = L0_ffn_w1, L0_ffn_w2, L0_ffn_w3

    def dram(name, shape):
        return nc.dram_tensor(name, shape, FP).ap()

    a.v_tok, a.s_tok = dram("v_tok_dram", [P, NB * S]), dram("s_tok_dram", [P, NB * S])
    a.logits = dram("logits_dram", [P, NB * NJ * 40])
    a.gate_rows = dram("gate_rows_dram", [2, NB, D])
    a.xh2 = dram("xh2_dram", [NB, S, D])
    a.route = dram("route_dram", [NB, E, S])
    a.band = dram("band_dram", [P, BAND])
    a.toeplitz_near, a.toeplitz_far = dram("toeplitz_near_dram", [P, D, P]), dram("toeplitz_far_dram", [C, D, C])
    a.window_near = bass.AP(a.band.tensor, P - 1, [[BAND, D], [-1, P], [1, P]])
    a.window_far = bass.AP(a.band.tensor, P - 1 + C, [[BAND, D], [-1, C], [1, C]])

    with ExitStack() as stack:
        k = Ctx(nc, stack)
        g.constants = k.sem("constants")
        g.toeplitz = k.sem("toeplitz")
        g.seqs = k.sb("seqs", [P, 4 * NB * S])
        g.ident, g.head_ones = k.sb("ident", [P, P]), k.sb("head_ones", [P, P])
        g.causal, g.pair_mask = k.sb("causal", [P, C]), k.sb("pair_mask", [P, C])
        g.item_mask = k.sb("item_mask", [P, G2 * NQ])
        g.eps_ln, g.eps_l2 = k.sb("eps_ln", [P, 1]), k.sb("eps_l2", [P, 1])
        g.full_s, g.row_step, g.row_base = k.sb("full_s", [P, 1]), k.sb("row_step", [P, NB // 2 - 1]), k.sb("row_base", [P, 2])
        g.mod, g.mod_slot = k.sb("mod", [P, 6, NB]), k.sb("mod_slot", [P, 2, NB])
        g.mod_flat = g.mod[:, :, :].rearrange("p k b -> p (k b)")
        g.mean, g.rstd = k.sb("mean", [P, NB * NJ]), k.sb("rstd", [P, NB * NJ])
        g.gb_rows = k.sb("gb_rows", [P, 2, 2, D])
        g.Wqkv = k.sb("Wqkv", [P, 3, D])
        g.Wb_wide = k.sb("Wb_wide", [P, D])
        Wb = k.sb("Wb", [P, NH])
        g.fus_W1, g.fus_W2 = k.sb("fus_W1", [P, NF]), k.sb("fus_W2", [P, 2, NH * NG])
        g.floor_W, g.Wo = k.sb("floor_W", [P, NH]), k.sb("Wo", [P, D])
        g.rw1, g.rw2 = k.sb("rw1", [P, RH]), k.sb("rw2", [RH, E])
        g.taps, g.w_short, g.w_long = k.sb("taps", [P, 3, TAPS]), k.sb("w_short", [P, FIR_S]), k.sb("w_long", [P, FIR_L])
        g.fus_b1, g.fus_b2, g.floor_b = k.sb("fus_b1", [P, 2]), k.sb("fus_b2", [P, NH * NG]), k.sb("floor_b", [P, NH])
        g.w_norm, g.pf_sq = k.sb("w_norm", [P, 3]), k.sb("pf_sq", [P, DH])
        g.slot_row, g.slot_w = k.sb("slot_row", [P, E, 4], U32), k.sb("slot_w", [P, E, 4])
        g.slot_row_flat = g.slot_row[:, :, :].rearrange("p e n -> p (e n)")
        g.slot_w_flat = g.slot_w[:, :, :].rearrange("p e n -> p (e n)")
        row = lambda w: w.rearrange("(o n) -> o n", o=1)
        col = lambda w: w.rearrange("(n o) -> n o", o=1)
        g.Wb = Wb
        g.weights = [
            (g.Wqkv[:, 0, :], L0_attn_Wq), (g.Wqkv[:, 1, :], L0_attn_Wk), (g.Wqkv[:, 2, :], L0_attn_Wv),
            (Wb[:, :], L0_attn_Wb), (g.fus_W1[:, :], L0_attn_fus_W1),
            (g.fus_W2[:, :, :], L0_attn_fus_W2.rearrange("(m p) n -> p m n", p=P)),
            (g.floor_W[:, :], L0_attn_floor_W), (g.Wo[:, :], L0_attn_Wo),
            (g.rw1[:, :], L0_ffn_router_w1), (g.rw2[:, :], L0_ffn_router_w2),
            (g.taps[:, 0, :], L0_attn_conv_q_w), (g.taps[:, 1, :], L0_attn_conv_k_w), (g.taps[:, 2, :], L0_attn_conv_v_w),
            (g.w_short[:, :], L0_attn_fir_short_w.rearrange("h d k -> (h d) k")),
            (g.w_long[:, :], L0_attn_fir_long_w.rearrange("h d k -> (h d) k")),
            (g.fus_b1[:, :], L0_attn_fus_b1.rearrange("(m p) -> p m", p=P)),
            (g.fus_b2[:, :], row(L0_attn_fus_b2).broadcast_to([P, NH * NG])),
            (g.floor_b[:, :], row(L0_attn_floor_b).broadcast_to([P, NH])),
            (g.pf_sq[:, :], row(L0_attn_norm_pf_w).broadcast_to([P, DH])),
        ] + [(g.w_norm[h * DH:(h + 1) * DH, n:n + 1], col(w)) for h in range(NH)
             for n, w in enumerate((L0_attn_norm_pf_w, L0_attn_norm_o_w))]
        stages = [stage_setup, stage_project, stage_delta, stage_fir]
        for n, stage in enumerate(stages):
            if n < upto:
                stage(nc, g, a)
        g.gate = [k.sb(f"gate{n}", [P, NB * NJ, NH]) for n in range(NG)]
        g.ga_rows = k.sb("ga_rows", [P, NB, D])
        for n, stage in enumerate([stage_gates, stage_mix, stage_route, stage_experts]):
            if n + 4 < upto:
                stage(nc, g, a)


_INS = ['L0_attn_hidden_states', 'L0_attn_Wq', 'L0_attn_Wk', 'L0_attn_Wv', 'L0_attn_Wb', 'L0_attn_conv_q_w',
        'L0_attn_conv_k_w', 'L0_attn_conv_v_w', 'L0_attn_fir_short_w', 'L0_attn_fir_long_w', 'L0_attn_floor_W',
        'L0_attn_floor_b', 'L0_attn_fus_W1', 'L0_attn_fus_b1', 'L0_attn_fus_W2', 'L0_attn_fus_b2',
        'L0_attn_norm_pf_w', 'L0_attn_norm_o_w', 'L0_attn_Wo', 'L0_ffn_router_w1', 'L0_ffn_router_w2',
        'L0_ffn_w1', 'L0_ffn_w2', 'L0_ffn_w3', 'L0_c', 'L0_wmod']
_OUTS = [((NB, S, D), 'float32')]


def kernel(**inputs):
    import numpy as _np
    import concourse.bacc as _bacc
    from concourse import mybir as _mybir
    from concourse.bass_utils import run_bass_kernel_spmd as _run

    nc = _bacc.Bacc("TRN2", target_bir_lowering=False, num_devices=1)
    arrays, args = {}, []
    for name in _INS:
        x = _np.ascontiguousarray(inputs[name])
        arrays[f"in_{name}_dram"] = x
        args.append(nc.dram_tensor(f"in_{name}_dram", x.shape, _mybir.dt.from_np(x.dtype), kind="ExternalInput").ap())
    for i, (shape, dtype) in enumerate(_OUTS):
        dt = _mybir.dt.from_np(_np.dtype(dtype))
        args.append(nc.dram_tensor(f"out_{i}_dram", shape, dt, kind="ExternalOutput").ap())
    adaln_block_kernel(nc, *args)
    r = _run(nc, [arrays], core_ids=[0])
    got = tuple(r.results[0][f"out_{i}_dram"] for i in range(len(_OUTS)))
    return got[0]
```

```python
from contextlib import ExitStack

import concourse.bass as bass
from concourse import mybir

FP = mybir.dt.float32
U32 = mybir.dt.uint32
ALU = mybir.AluOpType
ACT = mybir.ActivationFunctionType
AXX = mybir.AxisListType.X

P = 128
NB, S, D = 16, 512, 128
NH, DH = 8, 16
C = 32
NCH = S // C
NJ = S // P
TAPS, FIR_S, FIR_L = 4, 3, 31
NF = 256
NG = 4
E, DFF, CAP, RH = 16, 256, 32, 128
NQ, G2 = 4, 2
NI = NB * G2
BAND = 2 * P - 1
LN_EPS = RMS_EPS = 1e-5
L2_EPS = 1e-6
CMAX = 0.2
SA, CA, GA, SB_, CB, GB = range(6)
K_T, B_T, Q_T, V_T = range(4)
CHG = 8
NCG = D // CHG


def cut(t, start, n):
    return t[:, start:start + n] if isinstance(start, int) else t[:, bass.ds(start, n)]


def steps(eng, n, body, first=2):
    for t in range(first):
        body(t, t % 2)
    with eng.Fori(first // 2, n // 2) as i:
        for u in range(2):
            body(i * 2 + u, u)


def skewed(eng, n, parts):
    low, top = min(a for a, _ in parts), max(a for a, _ in parts)

    def round_(t, even):
        for ahead, part in parts:
            if not isinstance(t, int) or 0 <= t + ahead < n:
                part(t + ahead, (even + ahead) % 2)
    first, last = (3 - low) // 2 * 2, (n - top) // 2 * 2
    for t in range(-top, first):
        round_(t, t)
    with eng.Fori(first // 2, last // 2) as i:
        for u in range(2):
            round_(i * 2 + u, u)
    for t in range(last, n - low):
        round_(t, t)


def after(eng, sem, t, ago, per=1, at=None, alone=False):
    if isinstance(t, int) and t < ago:
        return
    eng.wait_ge(sem, (t - ago) * per + (per if at is None else at))
    if alone and not isinstance(t, int):
        eng.nop(nofuse=True)


def landed(eng, sems, t, u, dmas=1):
    eng.wait_ge(sems[u], (t - u + 2) * 8 * dmas)


class Ctx:

    def __init__(self, nc, stack):
        self.nc, self.stack = nc, stack

    def sb(self, name, shape, dt=FP):
        return self.stack.enter_context(self.nc.sbuf_tensor(name, shape, dt))

    def ps(self, name):
        return self.stack.enter_context(self.nc.psum_tensor(name, [P, 512], FP))

    def sem(self, name):
        return self.stack.enter_context(self.nc.semaphore(name))


def stage_setup(nc, g, a):
    DRAWN = 3 + 3 * NQ + NB // 2 - 1
    with ExitStack() as stack:
        k = Ctx(nc, stack)
        xt = g.seqs[:, V_T * NB * S:(V_T + 1) * NB * S]
        c_in = k.sb("c_in", [NB, D])
        c_act = k.sb("c_act", [D, NB])
        wmod = k.sb("wmod_sb", [D, 6 * D])
        stats = k.sb("stats", [P, NB * NJ, 6])
        spread = k.sb("spread", [P, NB * NJ])
        sign = k.sb("sign", [P, 2, NB])
        size = k.sb("size", [P, 2, NB])
        gates_row = k.sb("gates_row", [NB, 2, D])
        band = k.sb("band", [P, BAND])
        band_ready, band_out = k.sem("band_ready"), k.sem("band_out")
        ps_c, ps_mod, ps_row = k.ps("ps_c"), k.ps("ps_mod"), k.ps("ps_row")
        w_in, c_ready = k.sem("w_in"), k.sem("c_ready")
        x_in = [k.sem(f"x_in{n}") for n in range(4)]
        cleared, drawn, c_turned = k.sem("cleared"), k.sem("drawn"), k.sem("c_turned")
        mod_ready, dve_done, var_ready = k.sem("mod_ready"), k.sem("dve_done0"), k.sem("var_ready")
        gate_ready, row_ready, rows_moved = k.sem("gate_ready"), k.sem("row_ready"), k.sem("rows_moved")
        act_done = k.sem("act_done")
        SILU_DONE, GATE_ROWS_DONE, DEV_DONE = 1, 2, 3
        stat_done = k.sem("stat_done")
        block = stack.enter_context(nc.Block())

        @block.sync
        def _(sp):
            sp.dma_start(c_in[:, :], a.c).then_inc(c_ready, 16)
            sp.dma_start(wmod[:, :], a.wmod).then_inc(c_ready, 16)
            for n in range(4):
                sp.dma_start(xt[:, n * 2048:(n + 1) * 2048].rearrange("p (m d) -> p m d", d=D),
                             a.x[4 * n:4 * n + 4].rearrange("b (j p) d -> p (b j) d", p=P)).then_inc(x_in[n], 16)
            for dst, src in g.weights:
                sp.dma_start(dst, src, allow_slow_non_contiguous=True).then_inc(w_in, 16)
            sp.wait_ge(act_done, GATE_ROWS_DONE)
            sp.dma_start(a.gate_rows.rearrange("k b d -> b k d"), gates_row[:, :, :]).then_inc(rows_moved, 16)
            sp.wait_ge(rows_moved, 16)
            for bp in range(4):
                sp.dma_start(g.gb_rows[32 * bp:32 * bp + 32, :, :, :],
                             a.gate_rows[1].rearrange("(t h e) d -> h t e d", t=2, h=4)[bp:bp + 1]
                             .broadcast_to([32, 2, 2, D])).then_inc(rows_moved, 16)
            sp.wait_ge(band_ready, 2)
            sp.dma_start(a.band, band[:, :]).then_inc(band_out, 16)
            sp.wait_ge(rows_moved, 16 * 5)
            sp.wait_ge(band_out, 16)
            sp.wait_ge(w_in, 16 * len(g.weights))

        @block.scalar
        def _(act):
            act.wait_ge(c_turned, 1)
            act.activation(c_act[:, :], ps_c[:, 0:NB], ACT.Silu).then_inc(act_done, 1)
            act.wait_ge(row_ready, 1)
            act.activation(gates_row[:, :, :], ps_row[0:NB, 0:2 * D].rearrange("b (k d) -> b k d", k=2),
                           ACT.Copy).then_inc(act_done, 1)
            act.wait_ge(var_ready, 1)
            act.activation(spread[:, :], g.rstd[:, :], ACT.Sqrt, bias=g.eps_ln[:, :]).then_inc(act_done, 1)

        @block.gpsimd
        def _(pool):
            pool.memset(g.ident[:, :], 0.0).then_inc(cleared, 1)
            pool.memset(g.head_ones[:, :], 1.0).then_inc(cleared, 1)
            pool.memset(g.causal[:, :], 1.0).then_inc(cleared, 1)
            pool.memset(g.pair_mask[:, :], 1.0).then_inc(cleared, 1)
            pool.memset(g.eps_l2[:, :], L2_EPS).then_inc(cleared, 1)
            pool.memset(g.eps_ln[:, :], LN_EPS).then_inc(g.constants, 1)
            pool.wait_ge(cleared, 5)
            pool.wait_ge(g.constants, 1)
            count = 0

            def draw(out, src, op, fill, base, pattern, mult):
                nonlocal count
                pool.affine_select(out=out, in_=src, compare_op=op, fill=fill, base=base, pattern=pattern,
                                   channel_multiplier=mult).then_inc(drawn, 1)
                count += 1
                pool.wait_ge(drawn, count)

            draw(g.ident[:, :], g.ident[:, :], ALU.not_equal, 1.0, 0, [[-1, P]], 1)
            v = g.head_ones[:, :].rearrange("p (h d) -> p h d", d=DH)
            draw(v, v, ALU.is_ge, 0.0, 0, [[-DH, NH], [0, DH]], 1)
            draw(v, v, ALU.is_ge, 0.0, DH - 1, [[DH, NH], [0, DH]], -1)
            for q in range(NQ):
                r = g.causal[32 * q:32 * q + 32, :]
                draw(r, r, ALU.is_ge, 0.0, 0, [[1, C]], -1)
                r = g.pair_mask[32 * q:32 * q + 32, :].rearrange("p (g d) -> p g d", g=G2)
                draw(r, r, ALU.is_ge, 0.0, 0, [[-DH, G2], [0, DH]], 1)
                draw(r, r, ALU.is_ge, 0.0, DH - 1, [[DH, G2], [0, DH]], -1)
            pool.wait_ge(stat_done, 1)
            for n in range(1, NB // 2):
                draw(g.row_step[:, n - 1:n], g.full_s[:, :], ALU.is_ge, 0.0, -E * n, [[0, 1]], 1)
            assert count == DRAWN

        @block.tensor
        def _(pe):
            pe.wait_ge(c_ready, 32)
            pe.wait_ge(drawn, 1)
            pe.transpose(ps_c[:, 0:NB], c_in[:, :], g.ident[0:NB, 0:NB]).then_inc(c_turned, 1)
            pe.wait_ge(act_done, SILU_DONE)
            for n in range(6):
                last = pe.matmul(ps_mod[:, n * NB:(n + 1) * NB], wmod[:, n * D:(n + 1) * D], c_act[:, :],
                                 start=True, stop=True)
            last.then_inc(mod_ready, 1)
            pe.wait_ge(gate_ready, 1)
            for n, which in enumerate((GA, GB)):
                last = pe.transpose(ps_row[0:NB, n * D:(n + 1) * D], g.mod[:, which, :], g.ident[:, :])
            last.then_inc(row_ready, 1)

        @block.vector
        def _(dve):
            done = 0

            def then(ins):
                nonlocal done
                done += 1
                ins.then_inc(dve_done, 1)
                dve.wait_ge(dve_done, done)

            def stats_of(n):
                dve.wait_ge(x_in[n], 16)
                for m in range(16 * n, 16 * n + 16):
                    dve.bn_stats(stats[:, m, :], xt[:, m * D:(m + 1) * D]).then_inc(stat_done, 1)

            dve.memset(g.full_s[:, :], float(S)).then_inc(stat_done, 1)
            stats_of(0)
            dve.wait_ge(mod_ready, 1)
            then(dve.tensor_copy(g.mod[:, :, :], ps_mod[:, 0:6 * NB].rearrange("p (k b) -> p k b", b=NB)))
            pair = g.mod[:, GA:6:3, :]
            then(dve.tensor_scalar(g.mod[:, CA:6:3, :], g.mod[:, CA:6:3, :], 1.0, None, ALU.add))
            then(dve.tensor_scalar(sign[:, :, :], pair, 0.0, 2.0, ALU.is_ge, ALU.mult))
            then(dve.scalar_tensor_tensor(size[:, :, :], pair, -1.0, pair, ALU.mult, ALU.max))
            then(dve.tensor_scalar(size[:, :, :], size[:, :, :], 0.25, None, ALU.max))
            then(dve.scalar_tensor_tensor(pair, sign[:, :, :], -1.0, size[:, :, :], ALU.add, ALU.mult))
            for n, which in enumerate((CB, SB_)):
                src = g.mod[:, which, :].rearrange("p (t b e) -> p t e b", t=2, e=2)
                then(dve.tensor_copy(g.mod_slot[:, n, :].rearrange("p (t e b) -> p t e b", t=2, e=2), src))
            dve.engine_nop().then_inc(gate_ready, 1)
            for n in range(1, 4):
                stats_of(n)
            dve.wait_ge(stat_done, 1 + NB * NJ)
            then(dve.tensor_tensor(g.mean[:, :], stats[:, :, 1], stats[:, :, 4], ALU.add))
            then(dve.tensor_tensor(spread[:, :], stats[:, :, 1], stats[:, :, 4], ALU.subtract))
            then(dve.tensor_scalar(g.mean[:, :], g.mean[:, :], 0.5, None, ALU.mult))
            then(dve.tensor_tensor(spread[:, :], spread[:, :], spread[:, :], ALU.mult))
            then(dve.tensor_tensor(g.rstd[:, :], stats[:, :, 2], stats[:, :, 5], ALU.add))
            then(dve.tensor_scalar(spread[:, :], spread[:, :], 0.25, None, ALU.mult))
            then(dve.scalar_tensor_tensor(g.rstd[:, :], g.rstd[:, :], 1.0 / D, spread[:, :], ALU.mult, ALU.add))
            dve.wait_ge(g.constants, 1)
            dve.engine_nop().then_inc(var_ready, 1)
            dve.wait_ge(act_done, DEV_DONE)
            then(dve.reciprocal(g.rstd[:, :], spread[:, :]))
            dve.wait_ge(drawn, DRAWN)
            then(dve.reduce_sum(g.row_base[:, 0:1], g.row_step[:, :], AXX))
            then(dve.tensor_scalar(g.row_base[:, 1:2], g.row_base[:, 0:1], float(S * NB // 2), None, ALU.add))
            dve.memset(band[:, :], 0.0).then_inc(band_ready, 1)
            dve.wait_ge(band_ready, 1)
            dve.wait_ge(w_in, 16 * len(g.weights))
            dve.tensor_copy(band[:, P - FIR_L:P], g.w_long[:, :]).then_inc(band_ready, 1)
            dve.wait_ge(w_in, 16 * len(g.weights))
            then(dve.tensor_tensor(g.w_norm[:, 2:3], g.w_norm[:, 0:1], g.w_norm[:, 1:2], ALU.mult))
            then(dve.tensor_scalar(g.Wo[:, :], g.Wo[:, :], g.w_norm[:, 2:3], None, ALU.mult))
            then(dve.tensor_copy(g.Wb_wide[:, :].rearrange("p (h d) -> p h d", d=DH),
                                 g.Wb[:, :].unsqueeze(2).broadcast_to([P, NH, DH])))
            then(dve.tensor_tensor(g.pf_sq[:, :], g.pf_sq[:, :], g.pf_sq[:, :], ALU.mult))
            then(dve.tensor_scalar(g.pf_sq[:, :], g.pf_sq[:, :], RMS_EPS, None, ALU.add))


def stage_project(nc, g, a):
    with ExitStack() as stack:
        k = Ctx(nc, stack)
        N = S
        xh = k.sb("xh", [P, N])
        hT = [k.sb(f"hT{u}", [P, N]) for u in range(2)]
        padded = [k.sb(f"padded_{n}", [P, TAPS - 1 + N]) for n in "qkv"]
        conv = [k.sb(f"conv_{n}", [P, N]) for n in "qkv"]
        sq = [[k.sb(f"silu_{n}{u}", [P, (FIR_S - 1 if n == "v" else 0) + N]) for n in "qkv"] for u in range(2)]
        square = [k.sb(f"square_{n}", [P, N]) for n in "qk"]
        norm = k.sb("norm", [P, 2, NJ, NH])
        norm_wide = k.sb("norm_wide", [P, 2, NJ, D])
        beta = k.sb("beta", [P, N])
        hid = k.sb("hid", [P, 2, N])
        short = k.sb("short", [P, N])
        tok = [k.sb(f"tok_{n}", [P, N]) for n in "vs"]
        logit = k.sb("logit", [P, NJ * 40])
        ps_x = k.ps("ps_x")
        ps_p = [k.ps(f"ps_{n}") for n in "qkv"]
        ps_f = [k.ps(f"ps_f{n}") for n in range(2)]
        ps_a, ps_b = k.ps("ps_a"), k.ps("ps_b")
        names = """xh_done xT_ready hT_ready proj_q proj_k proj_v beta_logit fus_hidden pad_q pad_k pad_v
                   conv_q conv_k conv_v silu_q silu_k silu_v tanh_done beta_done square_q square_k sums
                   roots recips recips_wide wide_q wide_k q_done k_done b_done v_done gelu_done short_done v_turned s_turned
                   v_copied s_copied logit_ready logit_copied v_out s_out logit_out conv_step short_step cleared_pad""".split()
        s = {n: k.sem(n) for n in names}
        block = stack.enter_context(nc.Block())
        seq = lambda which, b: cut(g.seqs, b * S + which * NB * S, S)
        Q, K, V = range(3)
        ORDER = "kvq"

        @block.vector
        def _(dve):
            for n in range(3):
                dve.memset(padded[n][:, 0:TAPS - 1], 0.0).then_inc(s["cleared_pad"], 1)
            for u in range(2):
                dve.memset(sq[u][V][:, 0:FIR_S - 1], 0.0).then_inc(s["cleared_pad"], 1)
            dve.wait_ge(s["cleared_pad"], 5)

            def normalise(t, u):
                after(dve, s["xT_ready"], t, 1)
                for j in range(NJ):
                    m = t * NJ + j
                    last = dve.tensor_scalar(xh[:, j * P:(j + 1) * P], cut(g.seqs, m * D + V_T * NB * S, D),
                                             cut(g.mean, m, 1), cut(g.rstd, m, 1), ALU.subtract, ALU.mult)
                last.then_inc(s["xh_done"], 1)

            def convolve(t, n):
                i, done = "qkv".index(n), ORDER.index(n) * (TAPS - 1)
                after(dve, s["pad_" + n], t, 0)
                after(dve, s["silu_" + n], t, 1)
                for tap in range(TAPS):
                    if tap:
                        after(dve, s["conv_step"], t, 0, 3 * (TAPS - 1), done + tap)
                        ins = dve.scalar_tensor_tensor(conv[i][:, :], padded[i][:, tap:tap + N], g.taps[:, i, tap:tap + 1],
                                                       conv[i][:, :], ALU.mult, ALU.add)
                    else:
                        ins = dve.tensor_scalar(conv[i][:, :], padded[i][:, 0:N], g.taps[:, i, 0:1], None, ALU.mult)
                    ins.then_inc(s["conv_step"] if tap < TAPS - 1 else s["conv_" + n], 1)

            def finish(t, u):
                after(dve, s["tanh_done"], t, 0)
                dve.tensor_scalar(beta[:, :], beta[:, :], 0.5, 0.5, ALU.mult, ALU.add).then_inc(s["beta_done"], 1)
                after(dve, s["silu_v"], t, 0)
                after(dve, s["s_turned"], t, 1)
                for tap in range(FIR_S):
                    src = sq[u][V][:, tap:tap + N]
                    if tap:
                        after(dve, s["short_step"], t, 0, FIR_S - 1, tap)
                        ins = dve.scalar_tensor_tensor(short[:, :], src, g.w_short[:, tap:tap + 1], short[:, :], ALU.mult, ALU.add)
                    else:
                        ins = dve.tensor_scalar(short[:, :], src, g.w_short[:, 0:1], None, ALU.mult)
                    ins.then_inc(s["short_step"] if tap < FIR_S - 1 else s["short_done"], 1)

            def invert(t, u):
                after(dve, s["roots"], t, 0)
                dve.reciprocal(norm[:, :, :, :], norm[:, :, :, :]).then_inc(s["recips"], 1)
                after(dve, s["recips"], t, 0)
                after(dve, s["wide_q"], t, 1)
                wide = norm_wide[:, :, :, :].rearrange("p w j d -> p (w j d)").rearrange("p (n d) -> p n d", d=DH)
                dve.tensor_copy(wide, norm[:, :, :, :].rearrange("p w j h -> p (w j h)").unsqueeze(2)
                                .broadcast_to([P, 2 * NJ * NH, DH])).then_inc(s["recips_wide"], 1)

            def scale(t, u):
                after(dve, s["wide_k"], t, 0)
                dve.tensor_tensor(seq(K_T, t), sq[u][K][:, :], ps_b[:, :], ALU.mult).then_inc(s["k_done"], 1)
                after(dve, s["wide_q"], t, 0)
                dve.tensor_tensor(seq(Q_T, t), sq[u][Q][:, :], ps_a[:, :], ALU.mult).then_inc(s["q_done"], 1)
                after(dve, s["k_done"], t, 0)
                after(dve, s["beta_done"], t, 0)
                dve.scalar_tensor_tensor(seq(B_T, t), seq(K_T, t), -1.0, beta[:, :], ALU.mult, ALU.mult).then_inc(s["b_done"], 1)

            skewed(dve, NB, [(2, normalise), (1, lambda t, u: convolve(t, "k")), (1, lambda t, u: convolve(t, "v")),
                             (0, finish), (0, invert), (1, lambda t, u: convolve(t, "q")), (0, scale)])

        @block.gpsimd
        def _(pool):
            def body(t, u):
                after(pool, s["beta_done"], t, 0)
                after(pool, s["silu_v"], t, 0)
                after(pool, s["xh_done"], t, 0)
                pool.tensor_tensor(seq(V_T, t), sq[u][V][:, FIR_S - 1:], beta[:, :], ALU.mult).then_inc(s["v_done"], 1)
            steps(pool, NB, body)

        @block.scalar
        def _(act):
            act.wait_ge(s["cleared_pad"], 5)

            def modulate(t, u):
                after(act, s["xT_ready"], t, 0, alone=True)
                after(act, s["logit_ready"], t, 2, alone=True)
                act.activation(hT[u][:, :], ps_x[:, :], ACT.Identity, bias=cut(g.mod_flat, t + SA * NB, 1),
                               scale=cut(g.mod_flat, t + CA * NB, 1)).then_inc(s["hT_ready"], 1)

            def pad(t, n):
                i = "qkv".index(n)
                after(act, s["proj_" + n], t, 0, alone=True)
                after(act, s["conv_" + n], t, 1, alone=True)
                act.activation(padded[i][:, TAPS - 1:], ps_p[i][:, :], ACT.Copy).then_inc(s["pad_" + n], 1)

            def tanh(t, u):
                after(act, s["beta_logit"], t, 0, alone=True)
                after(act, s["b_done"], t, 1, alone=True)
                after(act, s["v_done"], t, 1, alone=True)
                act.activation(beta[:, :], ps_p[Q][:, :], ACT.Tanh, scale=0.5).then_inc(s["tanh_done"], 1)

            def silu(t, u, n):
                i = "qkv".index(n)
                after(act, s["conv_" + n], t, 0, alone=True)
                if i == V:
                    after(act, s["v_done"], t, 2, alone=True)
                    after(act, s["short_done"], t, 2, alone=True)
                    after(act, s["v_turned"], t, 2, alone=True)
                    dst = sq[u][V][:, FIR_S - 1:]
                else:
                    after(act, s[n + "_done"], t, 2, alone=True)
                    dst = sq[u][i][:, :]
                act.activation(dst, conv[i][:, :], ACT.Silu).then_inc(s["silu_" + n], 1)

            def squares(t, u):
                for i, n in ((K, "k"), (Q, "q")):
                    after(act, s["silu_" + n], t, 0, alone=True)
                    after(act, s["sums"], t, 1, alone=True)
                    act.activation(square[i][:, :], sq[u][i][:, :], ACT.Square).then_inc(s["square_" + n], 1)

            def gelu(t, u):
                after(act, s["fus_hidden"], t, 0, alone=True)
                after(act, s["logit_ready"], t, 1, alone=True)
                for m in range(2):
                    last = act.activation(hid[:, m, :], ps_f[m][:, :], ACT.Gelu, bias=g.fus_b1[:, m:m + 1])
                last.then_inc(s["gelu_done"], 1)

            def roots(t, u):
                after(act, s["sums"], t, 0, alone=True)
                after(act, s["wide_k"], t, 1, alone=True)
                act.activation(norm[:, :, :, :].rearrange("p w j h -> p (w j h)"), ps_a[:, 0:2 * NJ * NH], ACT.Sqrt,
                               bias=g.eps_l2[:, :]).then_inc(s["roots"], 1)

            def copy_turned(t, n):
                i, src = (0, ps_a) if n == "v" else (1, ps_b)
                after(act, s[n + "_turned"], t, 0, alone=True)
                after(act, s[n + "_out"], t, 1, 16, alone=True)
                act.activation(tok[i][:, :], src[:, :], ACT.Copy).then_inc(s[n + "_copied"], 1)

            def copy_logits(t, u):
                after(act, s["logit_ready"], t, 0, alone=True)
                after(act, s["logit_out"], t, 1, 16, alone=True)
                act.activation(logit[:, :], ps_b[:, 0:NJ * 40], ACT.Copy).then_inc(s["logit_copied"], 1)

            skewed(act, NB, [(0, lambda t, u: silu(t, u, "k")), (0, lambda t, u: silu(t, u, "q")), (0, tanh),
                             (0, squares), (1, lambda t, u: pad(t, "k")), (-1, lambda t, u: copy_turned(t, "v")),
                             (1, lambda t, u: pad(t, "v")), (0, lambda t, u: silu(t, u, "v")), (1, lambda t, u: pad(t, "q")),
                             (-1, lambda t, u: copy_turned(t, "s")), (0, gelu), (0, roots),
                             (0, copy_logits), (2, modulate)])

        @block.tensor
        def _(pe):
            def turn_x(t, u):
                after(pe, s["xh_done"], t, 0)
                after(pe, s["hT_ready"], t, 1)
                for j in range(NJ):
                    last = pe.transpose(ps_x[:, j * P:(j + 1) * P], xh[:, j * P:(j + 1) * P], g.ident[:, :])
                last.then_inc(s["xT_ready"], 1)

            def project(t, u):
                after(pe, s["hT_ready"], t, 0)
                for n in ORDER:
                    i = "qkv".index(n)
                    after(pe, s["pad_" + n], t, 1)
                    if i == Q:
                        after(pe, s["tanh_done"], t, 1)
                    pe.matmul(ps_p[i][:, :], g.Wqkv[:, i, :], hT[u][:, :], start=True, stop=True).then_inc(s["proj_" + n], 1)

            def beta_logits(t, u):
                after(pe, s["pad_q"], t, 0)
                pe.matmul(ps_p[Q][:, :], g.Wb_wide[:, :], hT[u][:, :], start=True, stop=True).then_inc(s["beta_logit"], 1)

            def fus_hidden(t, u):
                after(pe, s["gelu_done"], t, 1)
                for m in range(2):
                    last = pe.matmul(ps_f[m][:, :], g.fus_W1[:, m * P:(m + 1) * P], hT[u][:, :], start=True, stop=True)
                last.then_inc(s["fus_hidden"], 1)

            def reduce(t, u):
                after(pe, s["square_k"], t, 0)
                after(pe, s["square_q"], t, 0)
                after(pe, s["v_copied"], t, 1)
                for i in range(2):
                    for j in range(NJ):
                        col = (i * NJ + j) * NH
                        last = pe.matmul(ps_a[:, col:col + NH], square[i][:, j * P:(j + 1) * P], g.head_ones[:, 0:P:DH],
                                         start=True, stop=True)
                last.then_inc(s["sums"], 1)

            def logits(t, u):
                after(pe, s["s_copied"], t, 1)
                after(pe, s["gelu_done"], t, 0)
                for j in range(NJ):
                    rows = slice(j * P, (j + 1) * P)
                    pe.matmul(ps_b[:, 40 * j + 32:40 * j + 40], hT[u][:, rows], g.floor_W[:, :], start=True, stop=True)
                    for m in range(2):
                        last = pe.matmul(ps_b[:, 40 * j:40 * j + 32], hid[:, m, rows], g.fus_W2[:, m, :],
                                         start=(m == 0), stop=(m == 1))
                last.then_inc(s["logit_ready"], 1)

            def widen(t, u):
                after(pe, s["recips_wide"], t, 0)
                after(pe, s["logit_copied"], t, 0)
                for i, n, ps in ((K, "k", ps_b), (Q, "q", ps_a)):
                    for j in range(NJ):
                        last = pe.transpose(ps[:, j * P:(j + 1) * P], norm_wide[:, i, j, :], g.ident[:, :])
                    last.then_inc(s["wide_" + n], 1)

            def turn(t, u):
                after(pe, s["k_done"], t, 0)
                after(pe, s["short_done"], t, 0)
                for j in range(NJ):
                    last = pe.transpose(ps_b[:, j * P:(j + 1) * P], short[:, j * P:(j + 1) * P], g.ident[:, :])
                last.then_inc(s["s_turned"], 1)
                after(pe, s["q_done"], t, 0)
                after(pe, s["silu_v"], t, 0)
                for j in range(NJ):
                    last = pe.transpose(ps_a[:, j * P:(j + 1) * P],
                                        sq[u][V][:, FIR_S - 1 + j * P:FIR_S - 1 + (j + 1) * P], g.ident[:, :])
                last.then_inc(s["v_turned"], 1)

            skewed(pe, NB, [(1, project), (0, reduce), (1, beta_logits), (0, logits), (2, turn_x), (0, widen),
                            (1, fus_hidden), (0, turn)])

        @block.sync
        def _(sp):
            def store(t, u):
                after(sp, s["v_copied"], t, 0)
                sp.dma_start(cut(a.v_tok, t * N, N), tok[0][:, :]).then_inc(s["v_out"], 16)
                after(sp, s["s_copied"], t, 0)
                sp.dma_start(cut(a.s_tok, t * N, N), tok[1][:, :]).then_inc(s["s_out"], 16)

            def store_logits(t, u):
                after(sp, s["logit_copied"], t, 0)
                sp.dma_start(cut(a.logits, t * NJ * 40, NJ * 40), logit[:, :]).then_inc(s["logit_out"], 16)
            skewed(sp, NB, [(-1, store), (0, store_logits)])
            for n in ("v_out", "s_out", "logit_out"):
                sp.wait_ge(s[n], 16 * NB)


def stage_delta(nc, g, a):
    with ExitStack() as stack:
        k = Ctx(nc, stack)
        W = NB * C
        kv = k.sb("kv", [P, 2 * W])
        bq = [k.sb(f"bq{u}", [P, 2 * W]) for u in range(2)]
        k_wide = k.sb("k_wide", [P, NB, NQ, C])
        bq_heads = k.sb("bq_heads", [P, NB, G2, 2, C])
        k_tok, v_tok = k.sb("k_tok", [P, W]), k.sb("v_tok", [P, W])
        L = k.sb("L", [P, C, C])
        T = k.sb("T", [P, C, C])
        prod = k.sb("prod", [P, C * C // 4])
        TT = [k.sb(f"TT{u}", [P, NI * C]) for u in range(2)]
        attn = [k.sb(f"attn{u}", [P, NI, C]) for u in range(2)]
        r = k.sb("r", [P, W])
        uu = k.sb("u", [P, W])
        state = k.sb("state", [P, W])
        gain = k.sb("gain", [P, W])
        o_ch = k.sb("o_ch", [P, W])
        gram = stack.enter_context(nc.psum_tensor("gram", [P, NI * 2 * C], FP))
        ps_r, ps_u, ps_s, ps_o = k.ps("ps_r"), k.ps("ps_u"), k.ps("ps_s"), k.ps("ps_o")
        names = """wide_zero wide_in kv_in bq_in gram_ready L_ready attn_ready k_ready v_ready T_unit solved TT_ready
                   r_ps r_ready u_ps u_ready s_ps o_ps gain_ready state_ready o_turned o_stored unit_step""".split()
        s = {n: k.sem(n) for n in names}
        SOLVE = 2 * (C - 1)
        BEFORE_R, BEFORE_GAIN = 4, 22
        quad = lambda q: slice(32 * q, 32 * q + 32)
        block = stack.enter_context(nc.Block())

        def chunks(eng, run):
            run(0, 0, 2)
            run(1, 1, 2)
            with eng.Fori(1, NCH // 2 - 1) as i:
                run(i * 2, 0, 2)
                run(i * 2 + 1, 1, 2)
            run(NCH - 2, 0, 1)
            run(NCH - 1, 1, 0)

        @block.scalar
        def _(act):
            by_seq = g.seqs[:, :].rearrange("p (m s) -> p m s", s=S)
            wide = lambda x: x.rearrange("p (b c) -> p b c", c=C)
            act.wait_ge(s["wide_zero"], 1)

            def chunk_of(which, t):
                rows = by_seq[:, which * NB:(which + 1) * NB, :]
                return rows[:, :, t * C:(t + 1) * C] if isinstance(t, int) else rows[:, :, bass.ds(t * C, C)]

            def load_gram(t):
                after(act, s["gram_ready"], t, 1, alone=True)
                for q in range(NQ):
                    act.activation(k_wide[quad(q), :, q, :], chunk_of(K_T, t)[quad(q)], ACT.Copy)
                for w, which in enumerate((B_T, Q_T)):
                    for n in range(G2):
                        last = act.activation(bq_heads[:, :, n, w, :], chunk_of(which, t), ACT.Copy,
                                              scale=g.pair_mask[:, n * DH:n * DH + 1])
                last.then_inc(s["wide_in"], 1)

            def load(t, u):
                after(act, s["k_ready"], t, 1, alone=True)
                after(act, s["v_ready"], t, 1, alone=True)
                act.activation(wide(kv[:, 0:W]), chunk_of(K_T, t), ACT.Copy)
                act.activation(wide(kv[:, W:]), chunk_of(V_T, t), ACT.Copy).then_inc(s["kv_in"], 1)
                after(act, s["o_ps"], t, 2, alone=True)
                act.activation(wide(bq[u][:, 0:W]), chunk_of(B_T, t), ACT.Copy)
                act.activation(wide(bq[u][:, W:]), chunk_of(Q_T, t), ACT.Copy).then_inc(s["bq_in"], 1)

            def store(t):
                after(act, s["o_turned"], t, 0, alone=True)
                act.activation(chunk_of(V_T, t), wide(o_ch[:, :]), ACT.Copy).then_inc(s["o_stored"], 1)

            load_gram(0)
            load(0, 0)
            load_gram(1)

            def run(t, u, follow):
                if not (isinstance(t, int) and t == 0):
                    store(t - 1)
                if follow > 0:
                    load(t + 1, 1 - u)
                if follow > 1:
                    load_gram(t + 2)
                after(act, s["u_ps"], t, 0, alone=True)
                after(act, s["o_ps"], t, 1, alone=True)
                act.activation(uu[:, :], ps_u[:, :], ACT.Copy).then_inc(s["u_ready"], 1)
            chunks(act, run)
            store(NCH - 1)

        @block.gpsimd
        def _(pool):
            pool.memset(k_wide[:, :, :, :], 0.0).then_inc(s["wide_zero"], 1)

            def body(t, u):
                after(pool, s["TT_ready"], t, 1, alone=True)
                pool.memset(T[:, :, :], 0.0).then_inc(s["unit_step"], 1)
                after(pool, s["unit_step"], t, 0, alone=True)
                pool.memset(T[:, :, :].rearrange("p i j -> p (i j)")[:, 0:C * C:C + 1], 1.0).then_inc(s["T_unit"], 1)
            steps(pool, NCH, body)

        @block.tensor
        def _(pe):
            def make_gram(t, half):
                if half == 0:
                    after(pe, s["wide_in"], t, 0, alone=True)
                    after(pe, s["L_ready"], t, 1, alone=True)
                    after(pe, s["attn_ready"], t, 1, alone=True)
                for b in range(half * NB // 2, (half + 1) * NB // 2):
                    item = b * G2 * 2 * C
                    last = pe.matmul(gram[:, item:item + G2 * 2 * C], k_wide[:, b, :, :].rearrange("p q c -> p (q c)"),
                                     bq_heads[:, b, :, :, :].rearrange("p n w c -> p (n w c)"), start=True, stop=True)
                if half == 1:
                    last.then_inc(s["gram_ready"], 1)

            def per_pair(ps, lhs, rhs, only_first=False):
                for b in range(NB):
                    for q in range(NQ):
                        last = pe.matmul(ps[quad(q), b * C:(b + 1) * C], lhs[quad(q), b * C:(b + 1) * C],
                                         rhs[quad(q), b * C:(b + 1) * C], start=(b == 0 or not only_first),
                                         stop=not only_first, skip_group_check=only_first)
                return last

            def per_item(ps, lhs, rhs, add=False):
                for n in range(NI):
                    for q in range(NQ):
                        last = pe.matmul(ps[quad(q), n * DH:(n + 1) * DH], lhs[quad(q), n * C:(n + 1) * C],
                                         rhs[quad(q), n * DH:(n + 1) * DH], start=not add, stop=True,
                                         skip_group_check=add)
                return last

            for t in range(2):
                make_gram(t, 0)
                make_gram(t, 1)

            def run(t, u, follow):
                after(pe, s["bq_in"], t, 0, alone=True)
                after(pe, s["r_ready"], t, 1, alone=True)
                after(pe, s["state_ready"], t, 0, alone=True)
                per_pair(ps_r, bq[u][:, 0:W], state).then_inc(s["r_ps"], 1)
                after(pe, s["o_turned"], t, 1, alone=True)
                per_pair(ps_o, bq[u][:, W:], state, only_first=True)
                after(pe, s["TT_ready"], t, 0, alone=True)
                after(pe, s["u_ready"], t, 1, alone=True)
                after(pe, s["r_ready"], t, 0, alone=True)
                per_item(ps_u, TT[u], r).then_inc(s["u_ps"], 1)
                if follow > 1:
                    make_gram(t + 2, 0)
                after(pe, s["gain_ready"], t, 1, alone=True)
                after(pe, s["k_ready"], t, 0, alone=True)
                after(pe, s["u_ready"], t, 0, alone=True)
                per_pair(ps_s, k_tok, uu).then_inc(s["s_ps"], 1)
                after(pe, s["attn_ready"], t, 0, alone=True)
                per_item(ps_o, attn[u][:, :, :].rearrange("p n c -> p (n c)"), uu, add=True).then_inc(s["o_ps"], 1)
                if follow > 1:
                    make_gram(t + 2, 1)
            chunks(pe, run)

        @block.vector
        def _(dve):
            dve.memset(state[:, :], 0.0).then_inc(s["state_ready"], 1)
            g4 = gram[:, :].rearrange("p (n w i) -> p w i n", w=2, i=C)

            def turn_kv(t):
                after(dve, s["kv_in"], t, 0)
                after(dve, s["s_ps"], t, 1)
                dve.transpose(k_tok[:, :], kv[:, 0:W]).then_inc(s["k_ready"], 1)
                after(dve, s["r_ready"], t, 1)
                dve.transpose(v_tok[:, :], kv[:, W:]).then_inc(s["v_ready"], 1)

            def take_gram(t, u):
                after(dve, s["gram_ready"], t, 0)
                after(dve, s["solved"], t, 1, SOLVE)
                dve.transpose(L[:, :, :], g4[:, 0, :, :]).then_inc(s["L_ready"], 1)
                after(dve, s["o_ps"], t, 2)
                dve.tensor_tensor(attn[u][:, :, :], gram[:, :].rearrange("p (n w i) -> p n w i", w=2, i=C)[:, :, 1, :],
                                  g.causal[:, :].unsqueeze(1).broadcast_to([P, NI, C]), ALU.mult).then_inc(s["attn_ready"], 1)

            def solve(t, first, last):
                for m in range(first, last):
                    rows, cols = C - 1 - m, m + 1
                    tmp = prod[:, 0:rows * cols].rearrange("p (i j) -> p i j", j=cols)
                    if m == 0:
                        after(dve, s["L_ready"], t, 0)
                        after(dve, s["T_unit"], t, 0)
                    else:
                        after(dve, s["solved"], t, 0, SOLVE, 2 * m)
                    dve.tensor_tensor(tmp, L[:, m + 1:, m:m + 1].broadcast_to([P, rows, cols]),
                                      T[:, m:m + 1, 0:cols].broadcast_to([P, rows, cols]), ALU.mult).then_inc(s["solved"], 1)
                    after(dve, s["solved"], t, 0, SOLVE, 2 * m + 1)
                    dve.tensor_tensor(T[:, m + 1:, 0:cols], T[:, m + 1:, 0:cols], tmp, ALU.add).then_inc(s["solved"], 1)

            def turn_back(t, u):
                after(dve, s["solved"], t, 0, SOLVE)
                after(dve, s["u_ps"], t, 2)
                dve.transpose(TT[u][:, :].rearrange("p (n i) -> p i n", i=C), T[:, :, :]).then_inc(s["TT_ready"], 1)

            turn_kv(0)
            take_gram(0, 0)
            solve(0, 0, C - 1)
            turn_back(0, 0)

            def run(t, u, follow):
                if follow > 0:
                    take_gram(t + 1, 1 - u)
                    solve(t + 1, 0, BEFORE_R)
                after(dve, s["r_ps"], t, 0)
                after(dve, s["v_ready"], t, 0)
                after(dve, s["u_ps"], t, 1)
                dve.tensor_tensor(r[:, :], v_tok[:, :], ps_r[:, :], ALU.add).then_inc(s["r_ready"], 1)
                if follow > 0:
                    solve(t + 1, BEFORE_R, BEFORE_GAIN)
                after(dve, s["s_ps"], t, 0)
                dve.tensor_tensor(gain[:, :].rearrange("p (b c) -> p b c", c=C),
                                  ps_s[:, :].rearrange("p (b c) -> p b c", c=C),
                                  g.pair_mask[:, :].unsqueeze(1).broadcast_to([P, NB, C]), ALU.mult).then_inc(s["gain_ready"], 1)
                after(dve, s["gain_ready"], t, 0)
                dve.tensor_tensor(state[:, :], state[:, :], gain[:, :], ALU.add).then_inc(s["state_ready"], 1)
                if follow > 0:
                    solve(t + 1, BEFORE_GAIN, C - 1)
                    turn_back(t + 1, 1 - u)
                    turn_kv(t + 1)
                after(dve, s["o_ps"], t, 0)
                after(dve, s["o_stored"], t, 1)
                dve.transpose(o_ch[:, :], ps_o[:, :]).then_inc(s["o_turned"], 1)
            chunks(dve, run)


def stage_fir(nc, g, a):
    with ExitStack() as stack:
        k = Ctx(nc, stack)
        M = NB * NJ
        v_all = g.seqs[:, 0:M * D].rearrange("p (m d) -> p m d", d=D)
        y_all = g.seqs[:, M * D:2 * M * D].rearrange("p (m d) -> p m d", d=D)
        v_tail = g.seqs[0:C, Q_T * NB * S:(Q_T + 1) * NB * S].rearrange("p (m d) -> p m d", d=D)
        raw = k.sb("raw", [P, M, 40])
        z = k.sb("z", [P, M, NH, NG])
        zf = k.sb("zf", [P, M, NH])
        top = k.sb("top", [P, M, NH])
        near = [k.sb(f"near{u}", [P, CHG, P]) for u in range(2)]
        far = [k.sb(f"far{u}", [C, CHG, C]) for u in range(2)]
        near_lhs = [k.sb(f"near_lhs{u}", [P, CHG, P]) for u in range(2)]
        far_lhs = [k.sb(f"far_lhs{u}", [C, CHG, C]) for u in range(2)]
        v_step = [k.sb(f"v_step{u}", [P, CHG, M]) for u in range(2)]
        tail_step = [k.sb(f"tail_step{u}", [C, CHG, M]) for u in range(2)]
        ps = [k.ps(f"ps_y{u}") for u in range(2)]
        loaded, ga_in, exp3, exp_p, exp_f = k.sem("logits_in"), k.sem("ga_in"), k.sem("exp_ctx"), k.sem("exp_p"), k.sem("exp_floor")
        step, shifted, biased = k.sem("gate_step"), k.sem("shifted"), k.sem("biased")
        v_in, w_in = k.sem("v_in"), [k.sem(f"band_in{u}") for u in range(2)]
        mirrored, staged, tail_staged, y_ready, y_stored = k.sem("mirrored"), k.sem("staged"), k.sem("tail_staged"), k.sem("y_ready"), k.sem("y_stored")
        block = stack.enter_context(nc.Block())

        @block.sync
        def _(sp):
            sp.dma_start(raw[:, :, :], a.logits.rearrange("p (m c) -> p m c", c=40)).then_inc(loaded, 16)
            for n in range(4):
                cols = slice(n * M * D // 4, (n + 1) * M * D // 4)
                sp.dma_start(g.seqs[:, cols], a.v_tok[:, cols]).then_inc(v_in, 16)
            sp.dma_start(v_tail, a.v_tok[P - C:P, :].rearrange("p (m d) -> p m d", d=D)).then_inc(v_in, 16)

            def body(t, u):
                after(sp, mirrored, t, 2)
                rows = a.window_near[:, t * CHG:(t + 1) * CHG, :] if isinstance(t, int) else a.window_near[:, bass.ds(t * CHG, CHG), :]
                sp.dma_start(near[u][:, :, :], rows).then_inc(w_in[u], 16)
                rows = a.window_far[:, t * CHG:(t + 1) * CHG, :] if isinstance(t, int) else a.window_far[:, bass.ds(t * CHG, CHG), :]
                sp.dma_start(far[u][:, :, :], rows).then_inc(w_in[u], 16)
            steps(sp, NCG, body)
            sp.dma_start(g.ga_rows[:, :, :], a.gate_rows[0:1].broadcast_to([P, NB, D])).then_inc(ga_in, 16)
            sp.wait_ge(ga_in, 16)

        @block.gpsimd
        def _(pool):
            pool.wait_ge(v_in, 80)

            def body(t, u):
                after(pool, y_ready, t, 2)
                src = v_all[:, :, t * CHG:(t + 1) * CHG] if isinstance(t, int) else v_all[:, :, bass.ds(t * CHG, CHG)]
                pool.tensor_copy(v_step[u][:, :, :], src.rearrange("p m c -> p c m")).then_inc(staged, 1)
                src = v_tail[:, :, t * CHG:(t + 1) * CHG] if isinstance(t, int) else v_tail[:, :, bass.ds(t * CHG, CHG)]
                pool.tensor_copy(tail_step[u][:, :, :], src.rearrange("p m c -> p c m")).then_inc(tail_staged, 1)
            steps(pool, NCG, body)

        @block.vector
        def _(dve):
            done = 0

            def then(ins):
                nonlocal done
                done += 1
                ins.then_inc(step, 1)
                dve.wait_ge(step, done)

            dve.wait_ge(loaded, 16)
            dve.tensor_tensor(z[:, :, :, :].rearrange("p m h k -> p m (h k)"), raw[:, :, 0:32],
                              g.fus_b2[:, :].unsqueeze(1).broadcast_to([P, M, 32]), ALU.add).then_inc(biased, 1)
            dve.tensor_tensor(zf[:, :, :], raw[:, :, 32:40],
                              g.floor_b[:, :].unsqueeze(1).broadcast_to([P, M, NH]), ALU.add).then_inc(biased, 1)
            dve.wait_ge(biased, 2)
            then(dve.tensor_tensor(top[:, :, :], z[:, :, :, 0], z[:, :, :, 1], ALU.max))
            then(dve.tensor_tensor(top[:, :, :], top[:, :, :], z[:, :, :, 2], ALU.max))
            for n in range(3):
                then(dve.tensor_tensor(z[:, :, :, n], z[:, :, :, n], top[:, :, :], ALU.subtract))
            dve.engine_nop().then_inc(shifted, 1)
            dve.wait_ge(exp_f, 1)
            then(dve.tensor_scalar(zf[:, :, :], zf[:, :, :], 1.0, None, ALU.add))
            then(dve.reciprocal(zf[:, :, :], zf[:, :, :]))
            then(dve.tensor_scalar(zf[:, :, :], zf[:, :, :], -CMAX, 1.0, ALU.mult, ALU.add))
            dve.wait_ge(exp_p, 1)
            then(dve.tensor_scalar(top[:, :, :], z[:, :, :, 3], 1.0, None, ALU.add))
            then(dve.reciprocal(top[:, :, :], top[:, :, :]))
            then(dve.tensor_tensor(g.gate[3][:, :, :], zf[:, :, :], top[:, :, :], ALU.mult))
            dve.wait_ge(exp3, 1)
            then(dve.tensor_tensor(top[:, :, :], z[:, :, :, 0], z[:, :, :, 1], ALU.add))
            then(dve.tensor_tensor(top[:, :, :], top[:, :, :], z[:, :, :, 2], ALU.add))
            then(dve.reciprocal(top[:, :, :], top[:, :, :]))
            then(dve.tensor_scalar(zf[:, :, :], g.gate[3][:, :, :], -1.0, 1.0, ALU.mult, ALU.add))
            then(dve.tensor_tensor(top[:, :, :], top[:, :, :], zf[:, :, :], ALU.mult))
            for n in range(3):
                then(dve.tensor_tensor(g.gate[n][:, :, :], z[:, :, :, n], top[:, :, :], ALU.mult))

        @block.tensor
        def _(pe):
            def body(t, u):
                after(pe, mirrored, t, 0)
                after(pe, staged, t, 0)
                after(pe, tail_staged, t, 0)
                after(pe, y_stored, t, 2)
                for c in range(CHG):
                    out = ps[u][:, c * M:(c + 1) * M]
                    pe.matmul(out, near_lhs[u][:, c, :], v_step[u][:, c, :], start=True, stop=False, skip_group_check=True)
                    head = out[0:C, :].rearrange("p (b j) -> p b j", j=NJ)[:, :, 1:]
                    tail = tail_step[u][:, c, :].rearrange("p (b j) -> p b j", j=NJ)[:, :, 0:NJ - 1]
                    last = pe.matmul(head, far_lhs[u][:, c, :], tail, start=False, stop=True, skip_group_check=True)
                last.then_inc(y_ready, 1)
            steps(pe, NCG, body)

        @block.scalar
        def _(act):
            act.wait_ge(biased, 2)
            act.activation(z[:, :, :, 3], z[:, :, :, 3], ACT.Exp, scale=-1.0).then_inc(exp_p, 1)
            act.activation(zf[:, :, :], zf[:, :, :], ACT.Exp, scale=-1.0).then_inc(exp_f, 1)
            act.wait_ge(shifted, 1)
            act.activation(z[:, :, :, 0:3], z[:, :, :, 0:3], ACT.Exp).then_inc(exp3, 1)

            def mirror(t, u):
                landed(act, w_in, t, u, 2)
                after(act, y_ready, t, 2, alone=True)
                act.activation(near_lhs[u][:, :, :], near[u][:, :, ::-1], ACT.Copy)
                act.activation(far_lhs[u][:, :, :], far[u][:, :, ::-1], ACT.Copy).then_inc(mirrored, 1)

            def store(t, u):
                after(act, y_ready, t, 0, alone=True)
                dst = y_all[:, :, t * CHG:(t + 1) * CHG] if isinstance(t, int) else y_all[:, :, bass.ds(t * CHG, CHG)]
                act.activation(dst, ps[u][:, :].rearrange("p (c m) -> p m c", m=M), ACT.Copy).then_inc(y_stored, 1)
            skewed(act, NCG, [(1, mirror), (0, store)])


def stage_mix(nc, g, a):
    with ExitStack() as stack:
        k = Ctx(nc, stack)
        N, R = S, NJ * NH
        o_in = k.sb("o_in", [P, N])
        v_in = [k.sb(f"v_in{u}", [P, N]) for u in range(2)]
        s_in = [k.sb(f"s_in{u}", [P, N]) for u in range(2)]
        x_in = [k.sb(f"x_in{u}", [P, N]) for u in range(2)]
        acc = k.sb("acc", [P, N])
        part = k.sb("part", [P, N])
        side = k.sb("side", [P, N])
        side2 = k.sb("side2", [P, N])
        squares = k.sb("squares", [P, N])
        factor = k.sb("factor", [P, R])
        normed = k.sb("normed", [P, N])
        oT = k.sb("oT", [P, N])
        x1 = k.sb("x1", [P, N])
        st = k.sb("st", [P, NJ, 6])
        mv = k.sb("mv", [P, NJ, 2])
        dev = k.sb("dev", [P, NJ])
        xh = k.sb("xh2", [P, N])
        hT = k.sb("h2T", [P, N])
        rh = k.sb("rh", [P, N])
        lg = k.sb("lg", [E, N])
        ps_o, ps_t, ps_y, ps_h, ps_r1, ps_r2 = (k.ps(n) for n in ("pc_o", "pc_t", "pc_y", "pc_h", "pc_r1", "pc_r2"))
        names = """o_loaded o_turned side_ready acc_ready sums_ready factor_root factor_ready normed_ready var_ready dev_root dev_ready
                   n_turned oT_ready y_ready x1_ready x1_out xh_ready xh_out x_turned h_ready
                   r1_ready rh_ready r2_ready lg_ready lg_out dstep bstep pstep""".split()
        s = {n: k.sem("c_" + n) for n in names}
        vs_in, xs_in = ([k.sem(f"{n}_in{u}") for u in range(2)] for n in ("vs", "xs"))
        block = stack.enter_context(nc.Block())
        M = NB * NJ
        DCH = 6

        heads = lambda x: x.rearrange("p (r d) -> p r d", d=DH)
        tiles = lambda x: x.rearrange("p (j d) -> p j d", d=D)

        def weight(n, t):
            w = g.gate[n][:, :, :].rearrange("p m h -> p (m h)")
            return cut(w, t * R, R).unsqueeze(2).broadcast_to([P, R, DH])

        @block.sync
        def _(sp):
            def load_branches(t, u):
                after(sp, s["side_ready"], t, 2)
                sp.dma_start(v_in[u][:, :], cut(a.v_tok, t * N, N)).then_inc(vs_in[u], 16)
                sp.dma_start(s_in[u][:, :], cut(a.s_tok, t * N, N)).then_inc(vs_in[u], 16)

            def load_x(t, u):
                after(sp, s["x1_ready"], t, 2)
                src = a.x[t:t + 1] if isinstance(t, int) else a.x[bass.ds(t, 1)]
                sp.dma_start(tiles(x_in[u][:, :]), src.rearrange("b (j p) d -> p (b j) d", p=P)).then_inc(xs_in[u], 16)

            def store_x1(t, u):
                after(sp, s["x1_ready"], t, 0)
                dst = a.out[t:t + 1] if isinstance(t, int) else a.out[bass.ds(t, 1)]
                sp.dma_start(dst.rearrange("b (j p) d -> p (b j) d", p=P), tiles(x1[:, :])).then_inc(s["x1_out"], 16)

            def store_xh(t, u):
                after(sp, s["xh_ready"], t, 0)
                dst = a.xh2[t:t + 1] if isinstance(t, int) else a.xh2[bass.ds(t, 1)]
                sp.dma_start(dst.rearrange("b (j p) d -> p (b j) d", p=P), tiles(xh[:, :])).then_inc(s["xh_out"], 16)

            def store_logits(t, u):
                after(sp, s["lg_ready"], t, 0)
                dst = a.route[t:t + 1] if isinstance(t, int) else a.route[bass.ds(t, 1)]
                sp.dma_start(dst.rearrange("b e s -> e (b s)"), lg[:, :]).then_inc(s["lg_out"], 16)
            skewed(sp, NB, [(3, load_branches), (1, load_x), (-1, store_logits), (0, store_x1), (0, store_xh)])
            for n in ("x1_out", "xh_out", "lg_out"):
                sp.wait_ge(s[n], 16 * NB)

        @block.gpsimd
        def _(pool):
            def combine_side(t, u):
                landed(pool, vs_in, t, u, 2)
                after(pool, s["acc_ready"], t, 1)
                pool.tensor_tensor(heads(side[:, :]), heads(s_in[u][:, :]), weight(0, t), ALU.mult).then_inc(s["pstep"], 1)
                pool.tensor_tensor(heads(side2[:, :]), heads(v_in[u][:, :]), weight(3, t), ALU.mult).then_inc(s["pstep"], 1)
                after(pool, s["pstep"], t, 0, 2)
                pool.tensor_tensor(side[:, :], side[:, :], side2[:, :], ALU.add).then_inc(s["side_ready"], 1)
            skewed(pool, NB, [(2, combine_side)])

        @block.scalar
        def _(act):
            def load_o(t, u):
                after(act, s["o_turned"], t, 1, alone=True)
                act.activation(o_in[:, :], cut(g.seqs, t * S + V_T * NB * S, S), ACT.Copy).then_inc(s["o_loaded"], 1)

            def root_factor(t, u):
                after(act, s["sums_ready"], t, 0, alone=True)
                act.activation(factor[:, :], factor[:, :], ACT.Sqrt).then_inc(s["factor_root"], 1)

            def root_dev(t, u):
                after(act, s["var_ready"], t, 0, alone=True)
                act.activation(dev[:, :], mv[:, :, 1], ACT.Sqrt, bias=g.eps_ln[:, :]).then_inc(s["dev_root"], 1)

            def copy_oT(t, u):
                after(act, s["n_turned"], t, 0, alone=True)
                after(act, s["y_ready"], t, 1, alone=True)
                act.activation(oT[:, :], ps_t[:, :], ACT.Copy).then_inc(s["oT_ready"], 1)

            def route(t, u):
                after(act, s["x_turned"], t, 0, alone=True)
                after(act, s["r1_ready"], t, 1, alone=True)
                act.activation(hT[:, :], ps_h[:, :], ACT.Identity, bias=cut(g.mod_flat, t + SB_ * NB, 1),
                               scale=cut(g.mod_flat, t + CB * NB, 1)).then_inc(s["h_ready"], 1)
                after(act, s["r1_ready"], t, 0, alone=True)
                after(act, s["r2_ready"], t, 1, alone=True)
                act.activation(rh[:, :], ps_r1[:, :], ACT.Silu).then_inc(s["rh_ready"], 1)

            def copy_logits(t, u):
                after(act, s["r2_ready"], t, 0, alone=True)
                after(act, s["lg_out"], t, 1, 16, alone=True)
                act.activation(lg[:, :], ps_r2[0:E, :], ACT.Copy).then_inc(s["lg_ready"], 1)
            skewed(act, NB, [(1, root_factor), (0, root_dev), (-1, copy_logits), (2, load_o), (1, copy_oT), (0, route)])

        @block.tensor
        def _(pe):
            def turn(ps, src):
                for j in range(NJ):
                    last = pe.transpose(ps[:, j * P:(j + 1) * P], src[:, j * P:(j + 1) * P], g.ident[:, :])
                return last

            def turn_normed(t, u):
                after(pe, s["normed_ready"], t, 0)
                after(pe, s["oT_ready"], t, 1)
                turn(ps_t, normed).then_inc(s["n_turned"], 1)

            def turn_o(t, u):
                after(pe, s["o_loaded"], t, 0)
                after(pe, s["dstep"], t, 1, DCH, 1)
                turn(ps_o, o_in).then_inc(s["o_turned"], 1)

            def project(t, u):
                after(pe, s["oT_ready"], t, 0)
                after(pe, s["x1_ready"], t, 1)
                for j in range(NJ):
                    last = pe.matmul(ps_y[:, j * D:(j + 1) * D], oT[:, j * P:(j + 1) * P], g.Wo[:, :], start=True, stop=True)
                last.then_inc(s["y_ready"], 1)

            def route(t, u):
                after(pe, s["xh_ready"], t, 0)
                after(pe, s["h_ready"], t, 1)
                turn(ps_h, xh).then_inc(s["x_turned"], 1)
                after(pe, s["h_ready"], t, 0)
                after(pe, s["rh_ready"], t, 1)
                pe.matmul(ps_r1[:, :], g.rw1[:, :], hT[:, :], start=True, stop=True).then_inc(s["r1_ready"], 1)
                after(pe, s["rh_ready"], t, 0)
                after(pe, s["lg_ready"], t, 1)
                pe.matmul(ps_r2[0:E, :], g.rw2[:, :], rh[:, :], start=True, stop=True).then_inc(s["r2_ready"], 1)
            skewed(pe, NB, [(1, turn_normed), (2, turn_o), (1, project), (0, route)])

        @block.vector
        def _(dve):
            def combine(t, u):
                y_all = g.seqs[:, M * D:2 * M * D]
                count = 0

                def then(ins):
                    nonlocal count
                    count += 1
                    ins.then_inc(s["dstep"], 1)
                    after(dve, s["dstep"], t, 0, DCH, count)
                after(dve, s["normed_ready"], t, 1)
                after(dve, s["o_turned"], t, 0)
                then(dve.tensor_tensor(heads(acc[:, :]), heads(ps_o[:, :]), weight(2, t), ALU.mult))
                then(dve.tensor_tensor(heads(part[:, :]), heads(cut(y_all, t * N, N)), weight(1, t), ALU.mult))
                then(dve.tensor_tensor(acc[:, :], acc[:, :], part[:, :], ALU.add))
                after(dve, s["side_ready"], t, 0)
                dve.tensor_tensor(acc[:, :], acc[:, :], side[:, :], ALU.add).then_inc(s["acc_ready"], 1)
                after(dve, s["acc_ready"], t, 0)
                then(dve.tensor_tensor(squares[:, :], acc[:, :], acc[:, :], ALU.mult))
                then(dve.tensor_tensor(heads(squares[:, :]), heads(squares[:, :]),
                                       g.pf_sq[:, :].unsqueeze(1).broadcast_to([P, R, DH]), ALU.mult))
                then(dve.tensor_reduce(factor[:, :], heads(squares[:, :]), AXX, ALU.add))
                assert count == DCH
                dve.tensor_scalar(factor[:, :], factor[:, :], DH * RMS_EPS ** 2, None, ALU.add).then_inc(s["sums_ready"], 1)

            def scale(t, u):
                after(dve, s["factor_root"], t, 0)
                dve.reciprocal(factor[:, :], factor[:, :]).then_inc(s["factor_ready"], 1)
                after(dve, s["factor_ready"], t, 0)
                after(dve, s["n_turned"], t, 1)
                dve.scalar_tensor_tensor(heads(normed[:, :]), heads(acc[:, :]), DH ** 0.5,
                                         factor[:, :].unsqueeze(2).broadcast_to([P, R, DH]), ALU.mult, ALU.mult)\
                   .then_inc(s["normed_ready"], 1)

            def residual(t, u):
                after(dve, s["y_ready"], t, 0)
                after(dve, s["xh_ready"], t, 1)
                after(dve, s["x1_out"], t, 1, 16)
                landed(dve, xs_in, t, u)
                row = g.ga_rows[:, :, :].rearrange("p b d -> p (b d)")
                row = cut(row, t * D, D).unsqueeze(1).broadcast_to([P, NJ, D])
                b = s["bstep"]
                K = NJ + 1
                dve.tensor_tensor(tiles(x1[:, :]), tiles(ps_y[:, :]), row, ALU.mult).then_inc(b, 1)
                after(dve, b, t, 0, K, 1)
                dve.tensor_tensor(x1[:, :], x1[:, :], x_in[u][:, :], ALU.add).then_inc(s["x1_ready"], 1)
                after(dve, s["x1_ready"], t, 0)
                for j in range(NJ):
                    dve.bn_stats(st[:, j, :], x1[:, j * D:(j + 1) * D]).then_inc(b, 1)
                after(dve, b, t, 0, K, 1 + NJ, alone=True)
                for j in range(NJ):
                    last = dve.bn_aggr(mv[:, j, :], st[:, j, :])
                last.then_inc(s["var_ready"], 1)

            def normalise2(t, u):
                after(dve, s["dev_root"], t, 0)
                dve.reciprocal(dev[:, :], dev[:, :]).then_inc(s["dev_ready"], 1)
                after(dve, s["dev_ready"], t, 0)
                after(dve, s["x_turned"], t, 1)
                after(dve, s["xh_out"], t, 1, 16)
                for j in range(NJ):
                    last = dve.tensor_scalar(xh[:, j * D:(j + 1) * D], x1[:, j * D:(j + 1) * D], mv[:, j, 0:1],
                                             dev[:, j:j + 1], ALU.subtract, ALU.mult)
                last.then_inc(s["xh_ready"], 1)
            skewed(dve, NB, [(1, combine), (0, residual), (1, scale), (0, normalise2)])


def stage_route(nc, g, a):
    with ExitStack() as stack:
        k = Ctx(nc, stack)
        lg = k.sb("route_lg", [P, 2, S])
        work = k.sb("route_work", [P, 2, S])
        junk = k.sb("route_exp", [P, 2, S])
        best = k.sb("best", [P, 2, CAP])
        at = k.sb("at", [P, 2, CAP], U32)
        atf = k.sb("atf", [P, 2, CAP])
        neg = k.sb("neg", [P, 2])
        tot = k.sb("tot", [P, 2])
        rest = k.sb("rest", [P, 2])
        turned = k.sb("turned", [P, 2, CAP])
        loaded, step, neg_ready, exp_ready = k.sem("route_in"), k.sem("route_step"), k.sem("neg_ready"), k.sem("exp_ready")
        block = stack.enter_context(nc.Block())

        @block.sync
        def _(sp):
            for t in range(2):
                sp.dma_start(lg[:, t, :], a.route[8 * t:8 * t + 8].rearrange("b e s -> (b e) s")).then_inc(loaded, 16)
            sp.wait_ge(loaded, 32)

        @block.scalar
        def _(act):
            act.wait_ge(neg_ready, 1)
            for t in range(2):
                act.activation(junk[:, t, :], lg[:, t, :], ACT.Exp, bias=neg[:, t:t + 1], accum_out=tot[:, t:t + 1])
            for t in range(2):
                last = act.activation(best[:, t, :], best[:, t, :], ACT.Exp, bias=neg[:, t:t + 1])
            last.then_inc(exp_ready, 1)

        @block.vector
        def _(dve):
            done = 0

            def then(*ins):
                nonlocal done
                done += len(ins)
                for x in ins:
                    x.then_inc(step, 1)
                dve.wait_ge(step, done)

            dve.wait_ge(loaded, 32)
            for r in range(CAP // 8):
                cols = slice(8 * r, 8 * r + 8)
                src = [(lg if r == 0 else work)[:, t, :] for t in range(2)]
                then(*[dve.max(best[:, t, cols], src[t]) for t in range(2)])
                then(*[dve.max_index(at[:, t, cols], best[:, t, cols], src[t]) for t in range(2)])
                if r < CAP // 8 - 1:
                    then(*[dve.match_replace(work[:, t, :], best[:, t, cols], src[t], -3.0e38) for t in range(2)])
            then(dve.tensor_scalar(neg[:, :], best[:, :, 0], -1.0, None, ALU.mult))
            dve.engine_nop().then_inc(neg_ready, 1)
            then(dve.tensor_copy(atf[:, :, :], at[:, :, :]))
            then(*[dve.tensor_scalar(atf[:, t, :], atf[:, t, :], g.row_base[:, t:t + 1], None, ALU.add) for t in range(2)])
            then(*[dve.transpose(turned[:, t, :], atf[:, t, :]) for t in range(2)])
            then(dve.tensor_copy(g.slot_row[:, :, :].rearrange("p e (t b) -> p t b e", t=2),
                                 turned[:, :, :].rearrange("p t (b e) -> p t b e", b=2)))
            dve.wait_ge(exp_ready, 1)
            then(dve.reciprocal(tot[:, :], tot[:, :]))
            then(*[dve.tensor_scalar(best[:, t, :], best[:, t, :], tot[:, t:t + 1], None, ALU.mult) for t in range(2)])
            then(dve.reduce_sum(rest[:, :], best[:, :, :], AXX))
            then(dve.tensor_scalar(rest[:, :], rest[:, :], 1e-9, None, ALU.add))
            then(dve.reciprocal(rest[:, :], rest[:, :]))
            then(*[dve.tensor_scalar(best[:, t, :], best[:, t, :], rest[:, t:t + 1], None, ALU.mult) for t in range(2)])
            then(*[dve.transpose(turned[:, t, :], best[:, t, :]) for t in range(2)])
            then(dve.tensor_copy(g.slot_w[:, :, :].rearrange("p e (t b) -> p t b e", t=2),
                                 turned[:, :, :].rearrange("p t (b e) -> p t b e", b=2)))


def stage_experts(nc, g, a):
    with ExitStack() as stack:
        k = Ctx(nc, stack)
        N = NB * CAP
        NGR = N // P
        w1 = [k.sb(f"w1_{u}", [D, DFF]) for u in range(2)]
        w2 = [k.sb(f"w2_{u}", [D, DFF]) for u in range(2)]
        w3 = [k.sb(f"w3_{u}", [P, 2, D]) for u in range(2)]
        from_rows = [k.sb(f"from_rows{u}", [P, NGR], U32) for u in range(2)]
        to_rows = k.sb("to_rows", [P, NGR], U32)
        got = [k.sb(f"got{u}", [P, N]) for u in range(2)]
        xT = k.sb("xT", [P, N])
        gu = k.sb("gu", [P, 2, N])
        act_g = k.sb("act_g", [P, 2, N])
        y = [k.sb(f"y{u}", [P, N]) for u in range(2)]
        ps_x, ps_y = k.ps("pe_x"), k.ps("pe_y")
        ps_g = [k.ps(f"pe_g{m}") for m in range(2)]
        ps_v = [k.ps(f"pe_v{m}") for m in range(2)]
        names = """from_ready to_ready x_turned x_scaled x_ready gate_ready value_ready act_ready gu_ready y_ready
                   y_done added""".split()
        s = {n: k.sem("e_" + n) for n in names}
        w_in, got_in = ([k.sem(f"{n}_in{u}") for u in range(2)] for n in ("expert", "got"))
        block = stack.enter_context(nc.Block())
        groups = lambda x: x.rearrange("p (n c) -> p n c", c=CAP)
        flat_xh = a.xh2.rearrange("b s d -> (b s) d")
        flat_out = a.out.rearrange("b s d -> (b s) d")

        @block.sync
        def _(sp):
            def body(t, u):
                after(sp, s["y_ready"], t, 2)
                pick = lambda w: w[t:t + 1] if isinstance(t, int) else w[bass.ds(t, 1)]
                sp.dma_start(w1[u][:, :], pick(a.w1).rearrange("e d f -> d (e f)")).then_inc(w_in[u], 16)
                sp.dma_start(w2[u][:, :], pick(a.w2).rearrange("e d f -> d (e f)")).then_inc(w_in[u], 16)
                sp.dma_start(w3[u][:, :, :], pick(a.w3).rearrange("e (m p) d -> p (e m) d", p=P)).then_inc(w_in[u], 16)
            steps(sp, E, body)

        @block.gpsimd
        def _(pool):
            def gather(t, u):
                after(pool, s["x_turned"], t, 2, alone=True)
                pool.tensor_copy(from_rows[u][:, :], cut(g.slot_row_flat, t * NGR, NGR)).then_inc(s["from_ready"], 1)
                after(pool, s["from_ready"], t, 0, alone=True)
                for n in range(NGR):
                    pool.indirect_dma_start(got[u][:, n * D:(n + 1) * D], None, flat_xh,
                                            bass.IndirectOffsetOnAxis(ap=from_rows[u][:, n:n + 1], axis=0))\
                        .then_inc(got_in[u], 16)

            def add(t, u):
                after(pool, s["added"], t, 1, 16 * NGR, alone=True)
                pool.tensor_copy(to_rows[:, :], cut(g.slot_row_flat, t * NGR, NGR)).then_inc(s["to_ready"], 1)
                after(pool, s["to_ready"], t, 0, alone=True)
                after(pool, s["y_done"], t, 0, alone=True)
                for n in range(NGR):
                    pool.indirect_dma_start(flat_out, bass.IndirectOffsetOnAxis(ap=to_rows[:, n:n + 1], axis=0),
                                            y[u][:, n * D:(n + 1) * D], None, compute_op=ALU.add)\
                        .then_inc(s["added"], 16)
            skewed(pool, E, [(2, gather), (0, add)])
            pool.wait_ge(s["added"], 16 * NGR * E)

        @block.tensor
        def _(pe):
            def fetch(t, u):
                landed(pe, got_in, t, u, NGR)
                after(pe, s["x_scaled"], t, 1)
                for n in range(NGR):
                    last = pe.transpose(ps_x[:, n * P:(n + 1) * P], got[u][:, n * D:(n + 1) * D], g.ident[:, :])
                last.then_inc(s["x_turned"], 1)

            def run(t, u, last_step):
                after(pe, s["x_ready"], t, 0)
                landed(pe, w_in, t, u, 3)
                after(pe, s["act_ready"], t, 1)
                for m in range(2):
                    last = pe.matmul(ps_g[m][:, :], w1[u][:, m * P:(m + 1) * P], xT[:, :], start=True, stop=True)
                last.then_inc(s["gate_ready"], 1)
                after(pe, s["gu_ready"], t, 1)
                for m in range(2):
                    last = pe.matmul(ps_v[m][:, :], w2[u][:, m * P:(m + 1) * P], xT[:, :], start=True, stop=True)
                last.then_inc(s["value_ready"], 1)
                if not last_step:
                    fetch(t + 1, 1 - u)
                after(pe, s["gu_ready"], t, 0)
                after(pe, s["y_done"], t, 1)
                for n in range(NGR):
                    for m in range(2):
                        last = pe.matmul(ps_y[:, n * D:(n + 1) * D], gu[:, m, n * P:(n + 1) * P], w3[u][:, m, :],
                                         start=(m == 0), stop=(m == 1))
                last.then_inc(s["y_ready"], 1)
            fetch(0, 0)
            run(0, 0, False)
            run(1, 1, False)
            with pe.Fori(1, E // 2 - 1) as i:
                run(i * 2, 0, False)
                run(i * 2 + 1, 1, False)
            run(E - 2, 0, False)
            run(E - 1, 1, True)

        @block.scalar
        def _(act):
            def body(t, u):
                after(act, s["gate_ready"], t, 0, alone=True)
                after(act, s["gu_ready"], t, 1, alone=True)
                for m in range(2):
                    last = act.activation(act_g[:, m, :], ps_g[m][:, :], ACT.Silu)
                last.then_inc(s["act_ready"], 1)
            steps(act, E, body)

        @block.vector
        def _(dve):
            cb = g.mod_slot[:, 0, :].unsqueeze(2).broadcast_to([P, NB, CAP])
            sb = g.mod_slot[:, 1, :].unsqueeze(2).broadcast_to([P, NB, CAP])

            def modulate(t):
                after(dve, s["x_turned"], t, 0)
                after(dve, s["value_ready"], t, 1)
                dve.tensor_tensor(groups(xT[:, :]), groups(ps_x[:, :]), cb, ALU.mult).then_inc(s["x_scaled"], 1)
                after(dve, s["x_scaled"], t, 0)
                dve.tensor_tensor(groups(xT[:, :]), groups(xT[:, :]), sb, ALU.add).then_inc(s["x_ready"], 1)

            def body(t, u, last_step=False):
                after(dve, s["act_ready"], t, 0)
                after(dve, s["value_ready"], t, 0)
                after(dve, s["y_ready"], t, 1)
                for m in range(2):
                    last = dve.tensor_tensor(gu[:, m, :], act_g[:, m, :], ps_v[m][:, :], ALU.mult)
                last.then_inc(s["gu_ready"], 1)
                if not last_step:
                    modulate(t + 1)
                after(dve, s["y_ready"], t, 0)
                after(dve, s["added"], t, 2, 16 * NGR)
                for n in range(NGR):
                    last = dve.scalar_tensor_tensor(y[u][:, n * D:(n + 1) * D], ps_y[:, n * D:(n + 1) * D],
                                                    cut(g.slot_w_flat, t * NGR + n, 1),
                                                    g.gb_rows[:, n // 2, n % 2, :], ALU.mult, ALU.mult)
                last.then_inc(s["y_done"], 1)
            modulate(0)
            body(0, 0)
            body(1, 1)
            with dve.Fori(1, E // 2 - 1) as i:
                body(i * 2, 0)
                body(i * 2 + 1, 1)
            body(E - 2, 0)
            body(E - 1, 1, True)


class Part:
    pass


def adaln_block_kernel(nc, L0_attn_hidden_states, L0_attn_Wq, L0_attn_Wk, L0_attn_Wv, L0_attn_Wb, L0_attn_conv_q_w,
                       L0_attn_conv_k_w, L0_attn_conv_v_w, L0_attn_fir_short_w, L0_attn_fir_long_w, L0_attn_floor_W,
                       L0_attn_floor_b, L0_attn_fus_W1, L0_attn_fus_b1, L0_attn_fus_W2, L0_attn_fus_b2,
                       L0_attn_norm_pf_w, L0_attn_norm_o_w, L0_attn_Wo, L0_ffn_router_w1, L0_ffn_router_w2,
                       L0_ffn_w1, L0_ffn_w2, L0_ffn_w3, L0_c, L0_wmod, out):
    a, g = Part(), Part()
    a.x, a.c, a.wmod, a.out = L0_attn_hidden_states, L0_c, L0_wmod, out
    a.w1, a.w2, a.w3 = L0_ffn_w1, L0_ffn_w2, L0_ffn_w3

    def dram(name, shape):
        return nc.dram_tensor(name, shape, FP).ap()

    a.v_tok, a.s_tok = dram("v_tok_dram", [P, NB * S]), dram("s_tok_dram", [P, NB * S])
    a.logits = dram("logits_dram", [P, NB * NJ * 40])
    a.gate_rows = dram("gate_rows_dram", [2, NB, D])
    a.xh2 = dram("xh2_dram", [NB, S, D])
    a.route = dram("route_dram", [NB, E, S])
    a.band = dram("band_dram", [P, BAND])
    a.window_near = bass.AP(a.band.tensor, 0, [[1, P], [BAND, D], [1, P]])
    a.window_far = bass.AP(a.band.tensor, P - 2 * C, [[1, C], [BAND, D], [1, C]])

    with ExitStack() as stack:
        k = Ctx(nc, stack)
        g.constants = k.sem("constants")
        g.seqs = k.sb("seqs", [P, 4 * NB * S])
        g.ident, g.head_ones = k.sb("ident", [P, P]), k.sb("head_ones", [P, P])
        g.causal, g.pair_mask = k.sb("causal", [P, C]), k.sb("pair_mask", [P, C])
        g.eps_ln, g.eps_l2 = k.sb("eps_ln", [P, 1]), k.sb("eps_l2", [P, 1])
        g.full_s, g.row_step, g.row_base = k.sb("full_s", [P, 1]), k.sb("row_step", [P, NB // 2 - 1]), k.sb("row_base", [P, 2])
        g.mod, g.mod_slot = k.sb("mod", [P, 6, NB]), k.sb("mod_slot", [P, 2, NB])
        g.mod_flat = g.mod[:, :, :].rearrange("p k b -> p (k b)")
        g.mean, g.rstd = k.sb("mean", [P, NB * NJ]), k.sb("rstd", [P, NB * NJ])
        g.gb_rows = k.sb("gb_rows", [P, 2, 2, D])
        g.Wqkv = k.sb("Wqkv", [P, 3, D])
        g.Wb_wide = k.sb("Wb_wide", [P, D])
        Wb = k.sb("Wb", [P, NH])
        g.fus_W1, g.fus_W2 = k.sb("fus_W1", [P, NF]), k.sb("fus_W2", [P, 2, NH * NG])
        g.floor_W, g.Wo = k.sb("floor_W", [P, NH]), k.sb("Wo", [P, D])
        g.rw1, g.rw2 = k.sb("rw1", [P, RH]), k.sb("rw2", [RH, E])
        g.taps, g.w_short, g.w_long = k.sb("taps", [P, 3, TAPS]), k.sb("w_short", [P, FIR_S]), k.sb("w_long", [P, FIR_L])
        g.fus_b1, g.fus_b2, g.floor_b = k.sb("fus_b1", [P, 2]), k.sb("fus_b2", [P, NH * NG]), k.sb("floor_b", [P, NH])
        g.w_norm, g.pf_sq = k.sb("w_norm", [P, 3]), k.sb("pf_sq", [P, DH])
        g.slot_row, g.slot_w = k.sb("slot_row", [P, E, 4], U32), k.sb("slot_w", [P, E, 4])
        g.slot_row_flat = g.slot_row[:, :, :].rearrange("p e n -> p (e n)")
        g.slot_w_flat = g.slot_w[:, :, :].rearrange("p e n -> p (e n)")
        row = lambda w: w.rearrange("(o n) -> o n", o=1)
        col = lambda w: w.rearrange("(n o) -> n o", o=1)
        g.Wb = Wb
        g.weights = [
            (g.Wqkv[:, 0, :], L0_attn_Wq), (g.Wqkv[:, 1, :], L0_attn_Wk), (g.Wqkv[:, 2, :], L0_attn_Wv),
            (Wb[:, :], L0_attn_Wb), (g.fus_W1[:, :], L0_attn_fus_W1),
            (g.fus_W2[:, :, :], L0_attn_fus_W2.rearrange("(m p) n -> p m n", p=P)),
            (g.floor_W[:, :], L0_attn_floor_W), (g.Wo[:, :], L0_attn_Wo),
            (g.rw1[:, :], L0_ffn_router_w1), (g.rw2[:, :], L0_ffn_router_w2),
            (g.taps[:, 0, :], L0_attn_conv_q_w), (g.taps[:, 1, :], L0_attn_conv_k_w), (g.taps[:, 2, :], L0_attn_conv_v_w),
            (g.w_short[:, :], L0_attn_fir_short_w.rearrange("h d k -> (h d) k")),
            (g.w_long[:, :], L0_attn_fir_long_w.rearrange("h d k -> (h d) k")),
            (g.fus_b1[:, :], L0_attn_fus_b1.rearrange("(m p) -> p m", p=P)),
            (g.fus_b2[:, :], row(L0_attn_fus_b2).broadcast_to([P, NH * NG])),
            (g.floor_b[:, :], row(L0_attn_floor_b).broadcast_to([P, NH])),
            (g.pf_sq[:, :], row(L0_attn_norm_pf_w).broadcast_to([P, DH])),
        ] + [(g.w_norm[h * DH:(h + 1) * DH, n:n + 1], col(w)) for h in range(NH)
             for n, w in enumerate((L0_attn_norm_pf_w, L0_attn_norm_o_w))]
        stage_setup(nc, g, a)
        stage_project(nc, g, a)
        stage_delta(nc, g, a)
        g.gate = [k.sb(f"gate{n}", [P, NB * NJ, NH]) for n in range(NG)]
        g.ga_rows = k.sb("ga_rows", [P, NB, D])
        stage_fir(nc, g, a)
        stage_mix(nc, g, a)
        stage_route(nc, g, a)
        stage_experts(nc, g, a)


_INS = ['L0_attn_hidden_states', 'L0_attn_Wq', 'L0_attn_Wk', 'L0_attn_Wv', 'L0_attn_Wb', 'L0_attn_conv_q_w',
        'L0_attn_conv_k_w', 'L0_attn_conv_v_w', 'L0_attn_fir_short_w', 'L0_attn_fir_long_w', 'L0_attn_floor_W',
        'L0_attn_floor_b', 'L0_attn_fus_W1', 'L0_attn_fus_b1', 'L0_attn_fus_W2', 'L0_attn_fus_b2',
        'L0_attn_norm_pf_w', 'L0_attn_norm_o_w', 'L0_attn_Wo', 'L0_ffn_router_w1', 'L0_ffn_router_w2',
        'L0_ffn_w1', 'L0_ffn_w2', 'L0_ffn_w3', 'L0_c', 'L0_wmod']
_OUTS = [((NB, S, D), 'float32')]


def kernel(**inputs):
    import numpy as _np
    import concourse.bacc as _bacc
    from concourse import mybir as _mybir
    from concourse.bass_utils import run_bass_kernel_spmd as _run

    nc = _bacc.Bacc("TRN2", target_bir_lowering=False, num_devices=1)
    arrays, args = {}, []
    for name in _INS:
        x = _np.ascontiguousarray(inputs[name])
        arrays[f"in_{name}_dram"] = x
        args.append(nc.dram_tensor(f"in_{name}_dram", x.shape, _mybir.dt.from_np(x.dtype), kind="ExternalInput").ap())
    for i, (shape, dtype) in enumerate(_OUTS):
        dt = _mybir.dt.from_np(_np.dtype(dtype))
        args.append(nc.dram_tensor(f"out_{i}_dram", shape, dt, kind="ExternalOutput").ap())
    adaln_block_kernel(nc, *args)
    r = _run(nc, [arrays], core_ids=[0])
    got = tuple(r.results[0][f"out_{i}_dram"] for i in range(len(_OUTS)))
    return got[0]
```
